# Optimizing a Trainium2 kernel written in Bass

```python
import numpy as np
import jax
import jax.numpy as jnp

def _softmax(x, axis=-1):
    return jax.nn.softmax(x, axis=axis)

def _gelu(x):
    return jax.nn.gelu(x, approximate=True)

def _silu(x):
    return jax.nn.silu(x)

def _sigmoid(x):
    return jax.nn.sigmoid(x)

def _layernorm(x, axis=-1, eps=1e-05):
    m = jnp.mean(x, axis=axis, keepdims=True)
    v = jnp.var(x, axis=axis, keepdims=True)
    return (x - m) / jnp.sqrt(v + eps)

def _scatter_add(tgt, idx, src, axis=0):
    return tgt.at[idx].add(src)

def _segment_sum(src, seg, n):
    return jax.ops.segment_sum(src, seg, n)
kernel_name = 'mk_seq_preln_d1_jaxref_r8_f3d498'

def setup_inputs(seed: int=0):
    np.random.seed(seed)
    _w = jnp.asarray

    def _L0_attn_setup():
        import jax, jax.numpy as jnp
        import numpy as np
        DIM_IN, DIM_K, DIM_V, N_QUERY = (128, 128, 128, 8)

        def _kaiming_uniform(key, shape):
            fan_in = shape[-2] if len(shape) > 1 else shape[-1]
            gain = 1.0 / np.sqrt(3.0)
            bound = gain * np.sqrt(3.0 / fan_in)
            return jax.random.uniform(key, shape, jnp.float32, -bound, bound)
        key = jax.random.key(seed)
        kx, kq, kk, kv, ko = jax.random.split(key, 5)
        x = jax.random.normal(kx, (4, 256, DIM_IN), dtype=jnp.float32)
        proj_q = _kaiming_uniform(kq, (N_QUERY, DIM_IN, DIM_K))
        proj_k = _kaiming_uniform(kk, (DIM_IN, DIM_K))
        proj_v = _kaiming_uniform(kv, (DIM_IN, DIM_V))
        proj_o = _kaiming_uniform(ko, (N_QUERY, DIM_IN, DIM_V))
        return {'x': x, 'proj_q': proj_q, 'proj_k': proj_k, 'proj_v': proj_v, 'proj_o': proj_o}
    _L0_attn_in = _L0_attn_setup()

    def _L0_ffn_setup():
        import jax, jax.numpy as jnp
        import numpy as np
        EMBED = 128
        D_FF = 4 * EMBED
        N_EXPERTS = 8
        TOP_K = 2
        B, S = (2, 128)
        key = jax.random.key(seed)
        ks = jax.random.split(key, 10)
        sc_d = 1.0 / np.sqrt(EMBED)
        sc_h = 1.0 / np.sqrt(D_FF)
        return {'inputs': jax.random.normal(ks[0], (B, S, EMBED), jnp.float32), 'rw1': jax.random.normal(ks[1], (EMBED, D_FF), jnp.float32) * sc_d, 'rb1': jnp.zeros((D_FF,), jnp.float32), 'rw2': jax.random.normal(ks[2], (D_FF, N_EXPERTS), jnp.float32) * sc_h, 'rb2': jnp.zeros((N_EXPERTS,), jnp.float32), 'W1': jax.random.normal(ks[3], (N_EXPERTS, EMBED, D_FF), jnp.float32) * sc_d, 'b1': jnp.zeros((N_EXPERTS, D_FF), jnp.float32), 'W2': jax.random.normal(ks[4], (N_EXPERTS, D_FF, EMBED), jnp.float32) * sc_h, 'b2': jnp.zeros((N_EXPERTS, EMBED), jnp.float32)}
    _L0_ffn_in = _L0_ffn_setup()
    _d = {'L0_attn_x': _L0_attn_in['x'], 'L0_attn_proj_q': _L0_attn_in['proj_q'], 'L0_attn_proj_k': _L0_attn_in['proj_k'], 'L0_attn_proj_v': _L0_attn_in['proj_v'], 'L0_attn_proj_o': _L0_attn_in['proj_o'], 'L0_ffn_rw1': _L0_ffn_in['rw1'], 'L0_ffn_rb1': _L0_ffn_in['rb1'], 'L0_ffn_rw2': _L0_ffn_in['rw2'], 'L0_ffn_rb2': _L0_ffn_in['rb2'], 'L0_ffn_W1': _L0_ffn_in['W1'], 'L0_ffn_b1': _L0_ffn_in['b1'], 'L0_ffn_W2': _L0_ffn_in['W2'], 'L0_ffn_b2': _L0_ffn_in['b2']}
    _x0 = _d['L0_attn_x']
    _d['L0_attn_x'] = jax.random.normal(jax.random.fold_in(jax.random.key(seed), 1), (2, 2048, 128), dtype=_x0.dtype)
    del _x0
    return _d

def reference(L0_attn_x, L0_attn_proj_q, L0_attn_proj_k, L0_attn_proj_v, L0_attn_proj_o, L0_ffn_rw1, L0_ffn_rb1, L0_ffn_rw2, L0_ffn_rb2, L0_ffn_W1, L0_ffn_b1, L0_ffn_W2, L0_ffn_b2):

    def _L0_attn_ref(x, proj_q, proj_k, proj_v, proj_o):
        import jax, jax.numpy as jnp
        import numpy as np
        DIM_IN, DIM_K, DIM_V, N_QUERY = (128, 128, 128, 8)

        def _kaiming_uniform(key, shape):
            fan_in = shape[-2] if len(shape) > 1 else shape[-1]
            gain = 1.0 / np.sqrt(3.0)
            bound = gain * np.sqrt(3.0 / fan_in)
            return jax.random.uniform(key, shape, jnp.float32, -bound, bound)
        Q = jnp.einsum('bnd,hdk->bhnk', x, proj_q)
        K = jnp.einsum('bmd,dk->bmk', x, proj_k)
        V = jnp.einsum('bmd,dv->bmv', x, proj_v)
        logits = jnp.einsum('bhnk,bmk->bhnm', Q, K)
        weights = jax.nn.softmax(logits, axis=-1)
        O = jnp.einsum('bhnm,bmv->bhnv', weights, V)
        Y = jnp.einsum('bhnv,hdv->bnd', O, proj_o)
        return Y

    def _L0_ffn_ref(inputs, rw1, rb1, rw2, rb2, W1, b1, W2, b2):
        import jax, jax.numpy as jnp
        import numpy as np
        EMBED = 128
        D_FF = 4 * EMBED
        N_EXPERTS = 8
        TOP_K = 2
        B, S = (2, 128)
        Bb, Ss, D = inputs.shape
        T = Bb * Ss
        xf = inputs.reshape(T, D)
        score = jax.nn.relu(xf @ rw1 + rb1) @ rw2 + rb2
        _, topi = jax.lax.top_k(score, TOP_K)
        mask = jnp.zeros(score.shape, bool).at[jnp.arange(T)[:, None], topi].set(True)
        gate = jax.nn.softmax(jnp.where(mask, score, -jnp.inf), axis=-1)
        out = jnp.zeros_like(xf)
        for e in range(N_EXPERTS):
            h = jax.nn.relu(xf @ W1[e] + b1[e])
            y = h @ W2[e] + b2[e]
            out = out + gate[:, e:e + 1] * y
        return out.reshape(Bb, Ss, D)
    x = L0_attn_x
    x = x + _L0_attn_ref(_layernorm(x, axis=-1), L0_attn_proj_q, L0_attn_proj_k, L0_attn_proj_v, L0_attn_proj_o)
    x = x + _L0_ffn_ref(_layernorm(x, axis=-1), L0_ffn_rw1, L0_ffn_rb1, L0_ffn_rw2, L0_ffn_rb2, L0_ffn_W1, L0_ffn_b1, L0_ffn_W2, L0_ffn_b2)
    return x

_drawn_inputs = setup_inputs


def setup_inputs(seed=0):
    import zlib

    import numpy as np

    out = dict(_drawn_inputs(seed))
    spreads = {'L0_ffn_rb1': (0.0, 0.1),
     'L0_ffn_rb2': (0.0, 0.1),
     'L0_ffn_b1': (0.0, 0.1),
     'L0_ffn_b2': (0.0, 0.1)}
    factors = {}
    for name, (base, spread) in spreads.items():
        noise = np.random.default_rng([zlib.crc32(name.encode()), seed]).standard_normal(out[name].shape)
        drawn = base * np.exp(spread * noise) if base else spread * noise
        out[name] = jnp.asarray(drawn.astype(out[name].dtype))
    for name, factor in factors.items():
        out[name] = (out[name] * factor).astype(out[name].dtype)
    return out
```

```python
import numpy as np

B, N, D = 2, 2048, 128
HEADS = 8
P = 128
EPS = 1e-5
FF = 512
EXPERTS = 8
CH = 512
TPC = CH // P
TPB = N // P
CPB = N // CH
GPB = CPB * HEADS
TILES = B * TPB
CHUNKS = B * CPB
FT = FF // P
HI, LO = 0, 1
GR = 64


def attention(nc, t):
    import concourse.bass as bass
    from concourse import mybir
    from contextlib import ExitStack

    f32, f32r = mybir.dt.float32, mybir.dt.float32r
    ALU, ACT, AX = mybir.AluOpType, mybir.ActivationFunctionType, mybir.AxisListType
    ds = bass.ds
    x_sb, ident = t["x_sb"], t["ident"]

    with ExitStack() as ctx:
        def sb(name, shape, dt=f32):
            return ctx.enter_context(nc.sbuf_tensor(name, shape, dt))

        def pb(name, shape):
            return ctx.enter_context(nc.psum_tensor(name, shape, f32))

        def sem(name):
            return ctx.enter_context(nc.semaphore(name))

        probs = sb("probs", [P, 2, TPC, N])
        pt_hl = sb("pt_hl", [P, 4, 2, CH], f32r)
        xnT_hl = sb("xnT_hl", [P, 2, N], f32r)
        kT_hl = sb("kT_hl", [P, 2, N], f32r)
        v_hl = sb("v_hl", [P, 2, N], f32r)
        qT_hl = sb("qT_hl", [P, 2, 2, CH], f32r)
        oT_hl = sb("oT_hl", [P, 2, CH], f32r)
        wq_hl = sb("wq_hl", [P, HEADS, 2, D], f32r)
        wq_cur = sb("wq_cur", [P, 2, 2, D], f32r)
        wkv_hl = sb("wkv_hl", [P, 2, 2 * D], f32r)
        woT_hl = sb("woT_hl", [P, 2, HEADS * D], f32r)
        bn = sb("bn", [P, TPB, 6])
        mv = sb("mv", [P, TPB, 2])
        mhalf = sb("mhalf", [P, TPB])
        rstd = sb("rstd", [P, TPB])
        mx2 = sb("mx2", [P, 2])
        nmax = sb("nmax", [P, 2])
        sums = sb("sums", [P, 2, TPC, 2])
        rsum = sb("rsum", [P, TPC])
        rcp = sb("rcp", [P, 2, TPC])
        wq_raw = probs[:, 0, 1, 0:HEADS * D]
        wo_raw = probs[:, 0, 1, HEADS * D:2 * HEADS * D]
        wkv_raw = probs[:, 0, 2, 0:2 * D]
        xn = probs[:, 1, 0, :]

        sc = pb("sc", [P, N])
        tp = pb("tp", [P, 2, CH])
        ob = pb("ob", [P, 2, CH])

        s_x, s_w = sem("x_loaded"), sem("w_loaded")
        s_b2c, s_ffn = sem("b2_cleared"), sem("ffn_loaded")
        s_id0, s_id = sem("ident_cleared"), sem("ident_ready")
        s_mh = sem("mhalf_ready")
        s_pass = sem("passed")
        s_wqhi, s_wqlo = sem("wq_hi"), sem("wq_lo")
        s_wkhi, s_wklo = sem("wkv_hi"), sem("wkv_lo")
        s_wot, s_wohi, s_wolo = sem("wo_transposed"), sem("wo_hi"), sem("wo_lo")
        s_bn, s_mv, s_ve = sem("bn_stats"), sem("mean_var"), sem("var_eps")
        s_rstd, s_xn = sem("rstd_ready"), sem("xn_ready")
        s_xt, s_xhi, s_xlo = sem("xn_transposed"), sem("xnT_hi"), sem("xnT_lo")
        s_k, s_khi, s_klo = sem("k_done"), sem("k_hi"), sem("k_lo")
        s_v, s_vhi, s_vlo = sem("v_done"), sem("v_hi"), sem("v_lo")
        s_wc = sem("wq_cur_copied")
        s_q, s_qhi, s_qlo = sem("q_done"), sem("q_hi"), sem("q_lo")
        s_qk, s_mx, s_nm = sem("scores_done"), sem("half_max"), sem("max_ready")
        s_exp = sem("probs_ready")
        s_t, s_hi, s_lo = sem("probs_transposed"), sem("pt_hi"), sem("pt_lo")
        s_pv = sem("pv_done")
        s_ohi, s_olo = sem("o_hi"), sem("o_lo")
        s_y, s_yacc = sem("y_done"), sem("y_added")
        s_rs, s_rcp = sem("row_sums"), sem("rcp_ready")

        block = ctx.enter_context(nc.Block())

        @block.sync
        def _(sp):
            for b in range(B):
                if b > 0:
                    sp.wait_ge(s_x, 16 * b)
                sp.dma_start(x_sb[:, b * TPB:(b + 1) * TPB, :],
                             t["x"][b, :, :].rearrange("(n p) d -> p n d", p=P)).then_inc(s_x, 16)
            sp.dma_start(t["rw1_raw"][:, :], t["rw1"]).then_inc(s_ffn, 16)
            sp.dma_start(t["rw2_sb"][:, :, :], t["rw2"].rearrange("(f p) e -> p f e", p=P)).then_inc(s_ffn, 16)
            sp.dma_start(t["bias_raw"][0:EXPERTS * FT, :],
                         t["b1"].rearrange("e (f p) -> (e f) p", p=P)).then_inc(s_ffn, 16)
            sp.dma_start(t["bias_raw"][EXPERTS * FT:(EXPERTS + 1) * FT, :],
                         t["rb1"].rearrange("(f p) -> f p", p=P)).then_inc(s_ffn, 16)
            sp.dma_start(t["rb2_sb"][:, :], t["rb2"].rearrange("(e a) -> e a", a=1)).then_inc(s_ffn, 16)
            sp.wait_ge(s_b2c, 1)
            for row in (0, GR // 2):
                sp.dma_start(t["b2_raw"][row:row + EXPERTS, :], t["b2"]).then_inc(s_ffn, 16)
            sp.dma_start(t["w1_raw"][:, :, :], t["W1"].rearrange("e d f -> d e f")).then_inc(s_ffn, 16)
            sp.wait_ge(s_ffn, 8 * 16)

        @block.gpsimd
        def _(pool):
            pool.memset(ident[:, :], 0.0).then_inc(s_id0, 1)
            pool.memset(mhalf[:, :], -0.5).then_inc(s_mh, 1)
            pool.memset(t["b2_raw"][:, :], 0.0).then_inc(s_b2c, 1)
            pool.wait_ge(s_id0, 1)
            pool.affine_select(out=ident[:, :], in_=ident[:, :], compare_op=ALU.not_equal, fill=1.0,
                               base=0, pattern=[[-1, P]], channel_multiplier=1).then_inc(s_id, 1)
            pool.wait_ge(s_mh, 1)

            def copy_wq(head, parity):
                pool.tensor_copy(wq_cur[:, parity, :, :].rearrange("p a n -> p (a n)"),
                                 wq_hl[:, ds(head, 1), :, :].bitcast(f32)
                                 .rearrange("p h a n -> p (h a n)")).then_inc(s_wc, 1)

            def phase(G, head, parity):
                pool.wait_ge(s_q, G + 1)
                pool.sem_inc(s_pass, 1)
                copy_wq(head, parity)

            with pool.Fori(0, B) as b:
                pool.wait_ge(s_ve, b + 1)
                pool.tensor_tensor(rstd[:, :], mv[:, :, 1], mhalf[:, :], ALU.pow).then_inc(s_rstd, 1)
                pool.wait_ge(s_wqhi, 1)
                pool.wait_ge(s_wqlo, 1)
                copy_wq(0, 0)
                copy_wq(1, 1)
                phase(b * GPB, 2, 0)
                with pool.Fori(0, (GPB - 4) // 2) as i:
                    phase(b * GPB + i * 2 + 1, (i * 2 + 3) & (HEADS - 1), 1)
                    phase(b * GPB + i * 2 + 2, (i * 2 + 4) & (HEADS - 1), 0)
                phase(b * GPB + GPB - 3, HEADS - 1, 1)
                pool.wait_ge(s_q, (b + 1) * GPB)

        @block.scalar
        def _(act):
            act.dma_start(wkv_raw[:, 0:D], t["wk"]).then_inc(s_w, 16)
            act.dma_start(wkv_raw[:, D:2 * D], t["wv"]).then_inc(s_w, 16)
            act.dma_start(wq_raw.rearrange("p (h k) -> p h k", h=HEADS),
                          t["wq"].rearrange("h d k -> d h k")).then_inc(s_w, 16)
            act.dma_start(wo_raw.rearrange("p (h v) -> p h v", h=HEADS),
                          t["wo"].rearrange("h d v -> d h v")).then_inc(s_w, 16)
            act.wait_ge(s_w, 64)
            act.activation(wkv_hl[:, HI, :], wkv_raw, ACT.Copy).then_inc(s_wkhi, 1)
            act.activation(wq_hl[:, :, HI, :], wq_raw.rearrange("p (h k) -> p h k", h=HEADS),
                           ACT.Copy).then_inc(s_wqhi, 1)
            act.wait_ge(s_wot, 1)
            act.activation(woT_hl[:, HI, :], sc[:, 0:HEADS * D], ACT.Copy).then_inc(s_wohi, 1)

            def xt_hi(b, c):
                act.wait_ge(s_xt, b * CPB + c + 1)
                act.activation(xnT_hl[:, HI, c * CH:(c + 1) * CH], tp[:, c % 2, :],
                               ACT.Copy).then_inc(s_xhi, 1)

            def q_hi(G, k):
                act.wait_ge(s_q, G + 1)
                act.activation(qT_hl[:, k % 2, HI, :], ob[:, (k + 1) % 2, :], ACT.Copy).then_inc(s_qhi, 1)

            def exp_half(G, q, j, h):
                if h == 0:
                    act.wait_ge(s_nm, G * TPC + j + 1)
                act.activation(probs[:, q, j, h * (N // 2):(h + 1) * (N // 2)],
                               sc[:, h * (N // 2):(h + 1) * (N // 2)], ACT.Exp,
                               bias=nmax[:, j % 2:j % 2 + 1],
                               accum_out=sums[:, q, j, h:h + 1]).then_inc(s_exp, 1)

            def pt_hi(G, tile):
                act.wait_ge(s_t, G * TPB + tile + 1)
                act.activation(pt_hl[:, tile % 4, HI, :], tp[:, tile % 2, :], ACT.Copy).then_inc(s_hi, 1)

            def o_hi(G, p):
                act.wait_ge(s_pv, (G + 1) * TPB)
                act.activation(oT_hl[:, HI, :], ob[:, p, :], ACT.Copy).then_inc(s_ohi, 1)

            def phase(G, p, first=False, scores=True, queries=True):
                q = 1 - p
                for j in range(TPC):
                    def hi(tile):
                        if not (first and tile < 4):
                            act.wait_ge(s_pv, G * TPB + tile - 3)
                        pt_hi(G, tile)
                    hi(4 * j)
                    hi(4 * j + 1)
                    hi(4 * j + 2)
                    if scores:
                        if j == 0 and not first:
                            act.wait_ge(s_rcp, G)
                        exp_half(G + 1, q, j, 0)
                    hi(4 * j + 3)
                    if j == 0 and not first:
                        o_hi(G - 1, q)
                    if scores:
                        exp_half(G + 1, q, j, 1)
                    if j == 2 and queries:
                        q_hi(G + 2, p)

            with act.Fori(0, B) as b:
                xt_hi(b, 0)
                xt_hi(b, 1)
                for c in range(CPB):
                    act.wait_ge(s_k, b * CPB + c + 1)
                    act.activation(kT_hl[:, HI, c * CH:(c + 1) * CH], sc[:, c * CH:(c + 1) * CH],
                                   ACT.Copy).then_inc(s_khi, 1)
                    act.wait_ge(s_v, b * CPB + c + 1)
                    act.activation(v_hl[:, HI, c * CH:(c + 1) * CH], ob[:, c % 2, :],
                                   ACT.Copy).then_inc(s_vhi, 1)
                    if c + 2 < CPB:
                        xt_hi(b, c + 2)
                q_hi(b * GPB, 0)
                q_hi(b * GPB + 1, 1)
                for j in range(TPC):
                    exp_half(b * GPB, 0, j, 0)
                    exp_half(b * GPB, 0, j, 1)
                phase(b * GPB, 0, first=True)
                with act.Fori(0, (GPB - 4) // 2) as i:
                    phase(b * GPB + i * 2 + 1, 1)
                    phase(b * GPB + i * 2 + 2, 0)
                phase(b * GPB + GPB - 3, 1)
                phase(b * GPB + GPB - 2, 0, queries=False)
                phase(b * GPB + GPB - 1, 1, scores=False, queries=False)
                o_hi(b * GPB + GPB - 1, 1)

        @block.vector
        def _(dve):
            dve.wait_ge(s_w, 64)
            dve.wait_ge(s_wkhi, 1)
            dve.tensor_tensor(wkv_hl[:, LO, :], wkv_raw, wkv_hl[:, HI, :].bitcast(f32),
                              ALU.subtract).then_inc(s_wklo, 1)
            dve.wait_ge(s_wqhi, 1)
            dve.tensor_tensor(wq_hl[:, :, LO, :], wq_raw.rearrange("p (h k) -> p h k", h=HEADS),
                              wq_hl[:, :, HI, :].bitcast(f32), ALU.subtract).then_inc(s_wqlo, 1)
            dve.wait_ge(s_wohi, 1)
            dve.tensor_tensor(woT_hl[:, LO, :], sc[:, 0:HEADS * D], woT_hl[:, HI, :].bitcast(f32),
                              ALU.subtract).then_inc(s_wolo, 1)

            def low(out, psum, hi, done):
                dve.tensor_tensor(out, psum, hi.bitcast(f32), ALU.subtract).then_inc(done, 1)

            def xt_lo(b, c):
                dve.wait_ge(s_xhi, b * CPB + c + 1)
                cols = slice(c * CH, (c + 1) * CH)
                low(xnT_hl[:, LO, cols], tp[:, c % 2, :], xnT_hl[:, HI, cols], s_xlo)

            def q_lo(G, k):
                dve.wait_ge(s_qhi, G + 1)
                low(qT_hl[:, k % 2, LO, :], ob[:, (k + 1) % 2, :], qT_hl[:, k % 2, HI, :], s_qlo)

            def half_max(G, j, h):
                dve.wait_ge(s_qk, (G * TPC + j) * 2 + h + 1)
                dve.tensor_reduce(mx2[:, h:h + 1], sc[:, h * (N // 2):(h + 1) * (N // 2)], AX.X,
                                  ALU.max).then_inc(s_mx, 1)

            def neg_max(G, j):
                dve.wait_ge(s_mx, (G * TPC + j + 1) * 2)
                dve.tensor_reduce(nmax[:, j % 2:j % 2 + 1], mx2[:, :], AX.X, ALU.max,
                                  negate=True).then_inc(s_nm, 1)

            def pt_lo(G, tile):
                dve.wait_ge(s_hi, G * TPB + tile + 1)
                low(pt_hl[:, tile % 4, LO, :], tp[:, tile % 2, :], pt_hl[:, tile % 4, HI, :], s_lo)

            def o_lo(G, p):
                dve.wait_ge(s_ohi, G + 1)
                low(oT_hl[:, LO, :], ob[:, p, :], oT_hl[:, HI, :], s_olo)

            def reciprocals(G, p):
                dve.wait_ge(s_exp, (G + 1) * TPC * 2)
                dve.tensor_reduce(rsum[:, :], sums[:, p, :, :], AX.X, ALU.add).then_inc(s_rs, 1)
                dve.wait_ge(s_rs, G + 1)
                dve.reciprocal(rcp[:, p, :], rsum[:, :]).then_inc(s_rcp, 1)

            def y_add(G, p, tile0):
                dve.wait_ge(s_y, G + 1)
                for u in range(TPC):
                    tok = x_sb[:, ds(tile0 + u, 1), :].rearrange("p a d -> p (a d)")
                    last = dve.scalar_tensor_tensor(tok, ob[:, p, u * D:(u + 1) * D],
                                                    rcp[:, p, u:u + 1], tok, ALU.mult, ALU.add)
                last.then_inc(s_yacc, 1)

            def phase(G, p, tile0, first=False, scores=True, queries=True):
                q = 1 - p
                for j in range(TPC):
                    if scores:
                        half_max(G + 1, j, 0)
                    pt_lo(G, 4 * j)
                    pt_lo(G, 4 * j + 1)
                    if scores:
                        half_max(G + 1, j, 1)
                        neg_max(G + 1, j)
                    pt_lo(G, 4 * j + 2)
                    if j == 0:
                        reciprocals(G, p)
                    pt_lo(G, 4 * j + 3)
                    if j == 0 and not first:
                        o_lo(G - 1, q)
                    if j == 1 and not first:
                        y_add(G - 1, q, tile0)
                    if j == 2 and queries:
                        q_lo(G + 2, p)

            with dve.Fori(0, B) as b:
                dve.wait_ge(s_x, b * 16 + 16)
                for n in range(TPB):
                    last = dve.bn_stats(bn[:, n, :], x_sb[:, ds(b * TPB + n, 1), :]
                                        .rearrange("p a d -> p (a d)"))
                last.then_inc(s_bn, 1)
                dve.wait_ge(s_bn, b + 1)
                dve.sem_inc(s_pass, 1)
                for n in range(TPB):
                    last = dve.bn_aggr(mv[:, n, :], bn[:, n, :])
                last.then_inc(s_mv, 1)
                dve.wait_ge(s_mv, b + 1)
                dve.tensor_scalar(mv[:, :, 1], mv[:, :, 1], EPS, None, ALU.add).then_inc(s_ve, 1)
                dve.wait_ge(s_rstd, b + 1)
                for n in range(TPB):
                    ins = dve.tensor_scalar(xn[:, n * D:(n + 1) * D],
                                            x_sb[:, ds(b * TPB + n, 1), :].rearrange("p a d -> p (a d)"),
                                            mv[:, n, 0:1], rstd[:, n:n + 1], ALU.subtract, ALU.mult)
                    if n % TPC == TPC - 1:
                        ins.then_inc(s_xn, 1)
                xt_lo(b, 0)
                xt_lo(b, 1)
                for c in range(CPB):
                    cols = slice(c * CH, (c + 1) * CH)
                    dve.wait_ge(s_khi, b * CPB + c + 1)
                    low(kT_hl[:, LO, cols], sc[:, cols], kT_hl[:, HI, cols], s_klo)
                    dve.wait_ge(s_vhi, b * CPB + c + 1)
                    low(v_hl[:, LO, cols], ob[:, c % 2, :], v_hl[:, HI, cols], s_vlo)
                    if c + 2 < CPB:
                        xt_lo(b, c + 2)
                q_lo(b * GPB, 0)
                q_lo(b * GPB + 1, 1)
                for j in range(TPC):
                    half_max(b * GPB, j, 0)
                    half_max(b * GPB, j, 1)
                    neg_max(b * GPB, j)
                T0 = b * TPB
                last_chunk = TPB - TPC
                phase(b * GPB, 0, None, first=True)
                with dve.Fori(0, (GPB - 4) // 2) as i:
                    phase(b * GPB + i * 2 + 1, 1, T0 + (i & last_chunk))
                    phase(b * GPB + i * 2 + 2, 0, T0 + (i & last_chunk))
                phase(b * GPB + GPB - 3, 1, T0 + last_chunk)
                phase(b * GPB + GPB - 2, 0, T0 + last_chunk, queries=False)
                phase(b * GPB + GPB - 1, 1, T0 + last_chunk, scores=False, queries=False)
                o_lo(b * GPB + GPB - 1, 1)
                y_add(b * GPB + GPB - 1, 1, T0 + last_chunk)

        @block.tensor
        def _(pe):
            def product(out, lhs, rhs, start, stop):
                pe.matmul(out, lhs(HI), rhs(HI), start=start, stop=False)
                pe.matmul(out, lhs(HI), rhs(LO), start=False, stop=False)
                return pe.matmul(out, lhs(LO), rhs(HI), start=False, stop=stop)

            pe.wait_ge(s_id, 1)
            pe.wait_ge(s_w, 64)
            for h in range(HEADS):
                last = pe.transpose(sc[:, h * D:(h + 1) * D], wo_raw[:, h * D:(h + 1) * D], ident[:, :])
            last.then_inc(s_wot, 1)
            pe.wait_ge(s_wklo, 1)
            pe.wait_ge(s_wolo, 1)

            def xn_transposes(b, c):
                pe.wait_ge(s_xn, b * CPB + c + 1)
                if c >= 2:
                    pe.wait_ge(s_xlo, b * CPB + c - 1)
                for u in range(TPC):
                    n = c * TPC + u
                    last = pe.transpose(tp[:, c % 2, u * P:(u + 1) * P], xn[:, n * D:(n + 1) * D],
                                        ident[:, :])
                last.then_inc(s_xt, 1)

            def queries(G, k, col):
                pe.wait_ge(s_wc, G + 1)
                product(ob[:, (k + 1) % 2, :], lambda a: wq_cur[:, k % 2, a, :],
                        lambda a: xnT_hl[:, a, ds(col, CH)], True, True).then_inc(s_q, 1)

            def scores(G, q, j, c):
                if j == 0 and c == 0:
                    pe.wait_ge(s_qlo, G + 1)
                ins = product(sc[:, c * CH:(c + 1) * CH],
                              lambda a: qT_hl[:, q, a, j * P:(j + 1) * P],
                              lambda a: kT_hl[:, a, c * CH:(c + 1) * CH], True, True)
                if c % 2:
                    ins.then_inc(s_qk, 1)

            def transposes(G, p, tile, first):
                if tile == 0:
                    pe.wait_ge(s_exp, (G + 1) * TPC * 2)
                if not (first and tile < 2):
                    pe.wait_ge(s_lo, G * TPB + tile - 1)
                for u in range(TPC):
                    last = pe.transpose(tp[:, tile % 2, u * P:(u + 1) * P],
                                        probs[:, p, u, tile * P:(tile + 1) * P], ident[:, :])
                last.then_inc(s_t, 1)

            def pv(G, p, tile):
                pe.wait_ge(s_lo, G * TPB + tile + 1)
                product(ob[:, p, :], lambda a: v_hl[:, a, tile * D:(tile + 1) * D],
                        lambda a: pt_hl[:, tile % 4, a, :],
                        tile == 0, tile == TPB - 1).then_inc(s_pv, 1)

            def project(G, p, head):
                pe.wait_ge(s_olo, G + 1)
                for u in range(TPC):
                    last = product(ob[:, p, u * D:(u + 1) * D],
                                   lambda a: oT_hl[:, a, u * P:(u + 1) * P],
                                   lambda a: woT_hl[:, a, ds(head * D, D)], True, True)
                last.then_inc(s_y, 1)

            def phase(G, p, head, col, first=False, more=True, ask=True):
                q = 1 - p
                for j in range(TPC):
                    def sc4(c):
                        if more:
                            if c % 2 == 0:
                                pe.wait_ge(s_exp, ((G + 1) * TPC + j) * 2 - 1 + c // 2)
                            scores(G + 1, q, j, c)
                    sc4(0)
                    transposes(G, p, 4 * j, first)
                    sc4(1)
                    transposes(G, p, 4 * j + 1, first)
                    sc4(2)
                    sc4(3)
                    if j > 0:
                        pv(G, p, 4 * j - 2)
                    elif not first:
                        pv(G - 1, q, TPB - 2)
                    transposes(G, p, 4 * j + 2, first)
                    if j > 0:
                        pv(G, p, 4 * j - 1)
                    elif not first:
                        pv(G - 1, q, TPB - 1)
                    transposes(G, p, 4 * j + 3, first)
                    pv(G, p, 4 * j)
                    pv(G, p, 4 * j + 1)
                    if j == 1 and not first:
                        project(G - 1, q, head)
                    if j == 2 and ask:
                        if not first:
                            pe.wait_ge(s_yacc, G)
                        queries(G + 2, p, col)

            with pe.Fori(0, B) as b:
                xn_transposes(b, 0)
                xn_transposes(b, 1)
                for c in range(CPB):
                    cols = slice(c * CH, (c + 1) * CH)
                    pe.wait_ge(s_xlo, b * CPB + c + 1)
                    product(sc[:, cols], lambda a: wkv_hl[:, a, 0:D], lambda a: xnT_hl[:, a, cols],
                            True, True).then_inc(s_k, 1)
                    if c >= 2:
                        pe.wait_ge(s_vlo, b * CPB + c - 1)
                    for n in range(c * TPC, (c + 1) * TPC):
                        u = n % TPC
                        last = product(ob[:, c % 2, u * D:(u + 1) * D],
                                       lambda a: xnT_hl[:, a, n * P:(n + 1) * P],
                                       lambda a: wkv_hl[:, a, D:2 * D], True, True)
                    last.then_inc(s_v, 1)
                    if c + 2 < CPB:
                        xn_transposes(b, c + 2)
                pe.wait_ge(s_vlo, b * CPB + CPB)
                queries(b * GPB, 0, 0)
                queries(b * GPB + 1, 1, 0)
                for j in range(TPC):
                    for c in range(CPB):
                        if j > 0 and c % 2 == 0:
                            pe.wait_ge(s_exp, (b * GPB * TPC + j) * 2 - 1 + c // 2)
                        elif j == 0 and c % 2 == 0:
                            pe.wait_ge(s_klo, b * CPB + CPB)
                        scores(b * GPB, 0, j, c)
                phase(b * GPB, 0, None, 0, first=True)
                with pe.Fori(0, (GPB - 4) // 2) as i:
                    phase(b * GPB + i * 2 + 1, 1, (i * 2) & (HEADS - 1), ((i + 1) & (TPB - TPC)) * P)
                    phase(b * GPB + i * 2 + 2, 0, (i * 2 + 1) & (HEADS - 1), ((i + 2) & (TPB - TPC)) * P)
                phase(b * GPB + GPB - 3, 1, HEADS - 4, N - CH)
                phase(b * GPB + GPB - 2, 0, HEADS - 3, None, ask=False)
                phase(b * GPB + GPB - 1, 1, HEADS - 2, None, more=False, ask=False)
                pv(b * GPB + GPB - 1, 1, TPB - 2)
                pv(b * GPB + GPB - 1, 1, TPB - 1)
                project(b * GPB + GPB - 1, 1, HEADS - 1)


def experts(nc, t):
    import concourse.bass as bass
    from concourse import mybir
    from contextlib import ExitStack

    f32, f32r, u32 = mybir.dt.float32, mybir.dt.float32r, mybir.dt.uint32
    ALU, ACT, AX = mybir.AluOpType, mybir.ActivationFunctionType, mybir.AxisListType
    ds = bass.ds
    x_sb, ident = t["x_sb"], t["ident"]
    w1_raw, rw1_raw, rw2, bias_raw, rb2, b2_raw = (t[k] for k in (
        "w1_raw", "rw1_raw", "rw2_sb", "bias_raw", "rb2_sb", "b2_raw"))
    SLOTS = EXPERTS * FT
    LAG = 3
    NB = (EXPERTS + 1) * FT
    AT_XT, AT_R, AT_S, AT_ST, AT_GT = 6, (9, 10, 12, 13), 16, 18, 25

    with ExitStack() as ctx:
        def sb(name, shape, dt=f32):
            return ctx.enter_context(nc.sbuf_tensor(name, shape, dt))

        def pb(name, shape):
            return ctx.enter_context(nc.psum_tensor(name, shape, f32))

        def sem(name):
            return ctx.enter_context(nc.semaphore(name))

        w2_raw = sb("w2_raw", [P, EXPERTS, FF])
        w1_hl = sb("w1_hl", [P, 2, EXPERTS, FF], f32r)
        w2_hl = sb("w2_hl", [P, 2, EXPERTS, FF], f32r)
        rw1_hl = sb("rw1_hl", [P, 2, FF], f32r)
        b2_hl = sb("b2_hl", [GR, 2, D], f32r)
        biasT = sb("biasT", [P, NB])
        sel_f = sb("sel_f", [GR, EXPERTS, P])
        sel = sb("sel", [GR, EXPERTS, P], f32r)
        iota_u = sb("iota_u", [P, TPC, EXPERTS], mybir.dt.int32)
        iota = sb("iota", [P, TPC, EXPERTS])
        bn = sb("bn2", [P, TPC, 6])
        mv = sb("mv2", [P, TPC, 2])
        mhalf = sb("mhalf2", [P, TPC])
        rstd = sb("rstd2", [P, TPC])
        xn = sb("xn2", [P, CH])
        xT_hl = sb("xT_hl", [P, 2, 2, CH], f32r)
        rh = sb("rh", [P, FT, CH])
        sT = sb("sT", [EXPERTS, CH])
        s8 = sb("s8", [P, TPC, EXPERTS])
        top = sb("top", [P, TPC, 8])
        idx = sb("idx", [P, TPC, 8], u32)
        idxf = sb("idxf", [P, TPC, 8])
        is0 = sb("is0", [P, TPC, EXPERTS])
        is1 = sb("is1", [P, TPC, EXPERTS])
        mask = sb("mask", [P, TPC, EXPERTS])
        shifted = sb("shifted", [P, TPC, EXPERTS])
        e8 = sb("e8", [P, TPC, EXPERTS])
        em = sb("em", [P, TPC, EXPERTS])
        gsum = sb("gsum", [P, TPC])
        grcp = sb("grcp", [P, TPC])
        gpad = sb("gpad", [P, TPC, P])
        gT = sb("gT", [GR, 2, CH], f32r)
        gbc = sb("gbc", [P, 2, CH])
        tt = sb("tt", [P, 4, CH])
        h_hl = sb("h_hl", [P, 4, 2, CH], f32r)
        y_sb = sb("y_sb", [P, CH])

        zb = pb("zb", [P, 4, CH])
        yb = pb("yb", [P, CH])
        gb = pb("gb", [P, CH])
        mb = pb("mb", [P, 2, CH])

        s_dw2 = sem("w2_loaded")
        s_pad, s_se0, s_se1, s_sel = sem("gpad_cleared"), sem("sel_cleared"), sem("sel_half"), sem("sel_ready")
        s_iu, s_io, s_mh = sem("iota_made"), sem("iota_ready"), sem("mhalf_ready2")
        s_pass = sem("passed2")
        s_bt, s_bias = sem("bias_transposed"), sem("bias_ready")
        s_rwhi, s_rwlo = sem("rw1_hi"), sem("rw1_lo")
        s_b2hi, s_b2lo = sem("b2_hi"), sem("b2_lo")
        s_w1hi, s_w1lo, s_w2hi, s_w2lo = sem("w1_hi"), sem("w1_lo"), sem("w2_hi"), sem("w2_lo")
        s_bn, s_mv, s_ve, s_rstd, s_xn = (sem(n) for n in (
            "bn_stats2", "mean_var2", "var_eps2", "rstd_ready2", "xn_ready2"))
        s_xt, s_xhi, s_xlo = sem("x_transposed"), sem("xT_hi"), sem("xT_lo")
        s_r, s_rh, s_s, s_sT = sem("router_z"), sem("router_h"), sem("scores_done2"), sem("sT_ready")
        s_st, s_s8, s_top, s_idx, s_idf = (sem(n) for n in (
            "scores_transposed", "scores_ready", "top_ready", "idx_ready", "idxf_ready"))
        s_eq, s_mask, s_sh, s_e8, s_em, s_gs, s_gr, s_g = (sem(n) for n in (
            "equal_ready", "mask_ready", "shifted_ready", "gate_exp", "gate_masked", "gate_sum",
            "gate_rcp", "gates_ready"))
        s_gt, s_ghi, s_glo = sem("gates_transposed"), sem("gT_hi"), sem("gT_lo")
        s_gb, s_gbc = sem("gate_spread"), sem("gbc_ready")
        s_z, s_tt, s_hhi, s_hlo, s_w2 = (sem(n) for n in (
            "z_done", "tt_ready", "h_hi", "h_lo", "second_done"))
        s_y, s_ysb, s_yt, s_yadd = sem("y_chunk"), sem("y_in_sbuf"), sem("y_transposed"), sem("y_added2")
        s_out = sem("out_stored")

        block = ctx.enter_context(nc.Block())

        @block.sync
        def _(sp):
            sp.dma_start(w2_raw[:, :, :].rearrange("p e (f d) -> p (e f) d", f=FT),
                         t["W2"].rearrange("e (f p) d -> p (e f) d", p=P)).then_inc(s_dw2, 16)
            out = t["out"].rearrange("b n d -> (b n) d")
            with sp.Fori(0, CHUNKS) as c:
                sp.wait_ge(s_yadd, c + 1)
                sp.dma_start(out[ds(c * CH, CH), :].rearrange("(u p) d -> p u d", p=P),
                             x_sb[:, ds(c * TPC, TPC), :]).then_inc(s_out, 16)
            sp.wait_ge(s_out, 16 * CHUNKS)

        @block.gpsimd
        def _(pool):
            pool.memset(mhalf[:, :], -0.5).then_inc(s_mh, 1)
            pool.wait_ge(s_mh, 1)

            def power(c1):
                pool.wait_ge(s_ve, c1)
                pool.tensor_tensor(rstd[:, :], mv[:, :, 1], mhalf[:, :], ALU.pow).then_inc(s_rstd, 1)

            power(1)
            pool.memset(gpad[:, :, :], 0.0).then_inc(s_pad, 1)
            pool.memset(sel_f[:, :, :], 0.0).then_inc(s_se0, 1)
            for half, (before, after) in enumerate(((s_se0, s_se1), (s_se1, s_se1))):
                pool.wait_ge(before, 1)
                pool.affine_select(out=sel_f[:, :, :], in_=sel_f[:, :, :], compare_op=ALU.not_equal,
                                   fill=1.0, base=-32 * half, pattern=[[-1, EXPERTS], [0, P]],
                                   channel_multiplier=1).then_inc(after, 1)
            pool.wait_ge(s_se1, 2)
            pool.tensor_copy(sel[:, :, :], sel_f[:, :, :]).then_inc(s_sel, 1)
            pool.iota(iota_u[:, :, :], pattern=[[0, TPC], [1, EXPERTS]], base=0,
                      channel_multiplier=0).then_inc(s_iu, 1)
            pool.wait_ge(s_iu, 1)
            pool.tensor_copy(iota[:, :, :], iota_u[:, :, :]).then_inc(s_io, 1)
            for raw, hl, hi, lo in ((w1_raw, w1_hl, s_w1hi, s_w1lo), (w2_raw, w2_hl, s_w2hi, s_w2lo)):
                for e in range(EXPERTS):
                    pool.wait_ge(hi, e + 1)
                    pool.tensor_tensor(hl[:, LO, e, :], raw[:, e, :], hl[:, HI, e, :].bitcast(f32),
                                       ALU.subtract).then_inc(lo, 1)
            with pool.Fori(1, CHUNKS) as c:
                power(c + 1)

        @block.scalar
        def _(act):
            act.activation(rw1_hl[:, HI, :], rw1_raw[:, :], ACT.Copy).then_inc(s_rwhi, 1)
            act.activation(b2_hl[:, HI, :], b2_raw[:, :], ACT.Copy).then_inc(s_b2hi, 1)
            act.wait_ge(s_bt, 1)
            act.activation(biasT[:, :], gb[:, 0:NB], ACT.Copy).then_inc(s_bias, 1)
            act.wait_ge(s_bias, 1)

            def x_hi(C, q):
                act.wait_ge(s_xt, C + 1)
                act.activation(xT_hl[:, q, HI, :], mb[:, 0, :], ACT.Copy).then_inc(s_xhi, 1)

            def router_h(C, f):
                act.wait_ge(s_r, C * FT + f + 1)
                act.activation(rh[:, f, :], mb[:, (f + 1) % 2, :], ACT.Relu,
                               bias=biasT[:, EXPERTS * FT + f:EXPERTS * FT + f + 1]).then_inc(s_rh, 1)

            def score(C):
                act.wait_ge(s_s, C + 1)
                act.activation(sT[:, :], mb[0:EXPERTS, 1, :], ACT.Identity, bias=rb2[:, :]).then_inc(s_sT, 1)

            def gate_exp(C):
                act.wait_ge(s_sh, C + 1)
                act.activation(e8[:, :, :], shifted[:, :, :], ACT.Exp).then_inc(s_e8, 1)

            def gate_hi(C, q):
                act.wait_ge(s_gt, C + 1)
                act.activation(gT[:, q, :], mb[0:GR, 1, :], ACT.Copy).then_inc(s_ghi, 1)

            def gate_copy(C, e):
                act.wait_ge(s_gb, C * EXPERTS + e + 1)
                act.activation(gbc[:, e % 2, :], gb[:, :], ACT.Copy).then_inc(s_gbc, 1)

            x_hi(0, 0)
            for e in range(EXPERTS):
                act.activation(w1_hl[:, HI, e, :], w1_raw[:, e, :], ACT.Copy).then_inc(s_w1hi, 1)
            for f in range(FT):
                router_h(0, f)
            score(0)
            act.wait_ge(s_dw2, 16)
            for e in range(EXPERTS):
                act.activation(w2_hl[:, HI, e, :], w2_raw[:, e, :], ACT.Copy).then_inc(s_w2hi, 1)
            gate_exp(0)
            gate_hi(0, 0)
            gate_copy(0, 0)

            def phase(C, p, prep=True, first=False):
                q = 1 - p
                for k in range(SLOTS):
                    act.wait_ge(s_tt, C * SLOTS + k + 1)
                    if not (first and k < 4):
                        act.wait_ge(s_w2, C * SLOTS + k - 3)
                    act.activation(h_hl[:, k % 4, HI, :], tt[:, k % 4, :], ACT.Relu).then_inc(s_hhi, 1)
                    if k % FT == 1 and k + FT < SLOTS:
                        gate_copy(C, k // FT + 1)
                    if k == 2 and not first:
                        act.wait_ge(s_y, C)
                        act.activation(y_sb[:, :], yb[:, :], ACT.Copy).then_inc(s_ysb, 1)
                    if prep:
                        if k == AT_XT + 1:
                            x_hi(C + 1, q)
                        for f in range(FT):
                            if k == AT_R[f] + 1:
                                router_h(C + 1, f)
                        if k == AT_S + 2:
                            score(C + 1)
                        if k == AT_ST + 3:
                            gate_exp(C + 1)
                        if k == AT_GT + 1:
                            gate_hi(C + 1, q)
                        if k == SLOTS - 1:
                            gate_copy(C + 1, 0)

            phase(0, 0, first=True)
            with act.Fori(0, (CHUNKS - 2) // 2) as i:
                phase(i * 2 + 1, 1)
                phase(i * 2 + 2, 0)
            phase(CHUNKS - 1, 1, prep=False)
            act.wait_ge(s_y, CHUNKS)
            act.activation(y_sb[:, :], yb[:, :], ACT.Copy).then_inc(s_ysb, 1)

        @block.vector
        def _(dve):
            def low(out, x, hi, done):
                dve.tensor_tensor(out, x, hi.bitcast(f32), ALU.subtract).then_inc(done, 1)

            def tile(C, u):
                return x_sb[:, ds(C * TPC + u, 1), :].rearrange("p a d -> p (a d)")

            def moments(C):
                for u in range(TPC):
                    last = dve.bn_stats(bn[:, u, :], tile(C, u))
                last.then_inc(s_bn, 1)
                dve.wait_ge(s_bn, C + 1)
                dve.sem_inc(s_pass, 1)
                for u in range(TPC):
                    last = dve.bn_aggr(mv[:, u, :], bn[:, u, :])
                last.then_inc(s_mv, 1)
                dve.wait_ge(s_mv, C + 1)
                dve.tensor_scalar(mv[:, :, 1], mv[:, :, 1], EPS, None, ALU.add).then_inc(s_ve, 1)

            def normalise(C):
                dve.wait_ge(s_rstd, C + 1)
                for u in range(TPC):
                    last = dve.tensor_scalar(xn[:, u * D:(u + 1) * D], tile(C, u), mv[:, u, 0:1],
                                             rstd[:, u:u + 1], ALU.subtract, ALU.mult)
                last.then_inc(s_xn, 1)

            def x_lo(C, q):
                dve.wait_ge(s_xhi, C + 1)
                low(xT_hl[:, q, LO, :], mb[:, 0, :], xT_hl[:, q, HI, :], s_xlo)

            def over(a):
                return a.to_broadcast([P, TPC, EXPERTS])

            def top_two(C):
                dve.wait_ge(s_st, C + 1)
                dve.tensor_copy(s8[:, :, :], mb[:, 0, 0:TPC * EXPERTS]
                                .rearrange("p (u e) -> p u e", u=TPC)).then_inc(s_s8, 1)
                dve.wait_ge(s_s8, C + 1)
                dve.sem_inc(s_pass, 1)
                for u in range(TPC):
                    last = dve.max(top[:, u, :], s8[:, u, :])
                last.then_inc(s_top, 1)
                dve.wait_ge(s_top, C + 1)
                dve.tensor_tensor(shifted[:, :, :], s8[:, :, :], over(top[:, :, 0:1]),
                                  ALU.subtract).then_inc(s_sh, 1)
                for u in range(TPC):
                    last = dve.max_index(idx[:, u, :], top[:, u, :], s8[:, u, :])
                last.then_inc(s_idx, 1)
                dve.wait_ge(s_idx, C + 1)
                dve.tensor_copy(idxf[:, :, :], idx[:, :, :]).then_inc(s_idf, 1)
                dve.wait_ge(s_idf, C + 1)
                dve.tensor_tensor(is0[:, :, :], iota[:, :, :], over(idxf[:, :, 0:1]), ALU.is_equal)
                dve.tensor_tensor(is1[:, :, :], iota[:, :, :], over(idxf[:, :, 1:2]),
                                  ALU.is_equal).then_inc(s_eq, 1)
                dve.wait_ge(s_eq, C + 1)
                dve.tensor_tensor(mask[:, :, :], is0[:, :, :], is1[:, :, :], ALU.add).then_inc(s_mask, 1)

            def gates(C):
                dve.wait_ge(s_e8, C + 1)
                dve.wait_ge(s_mask, C + 1)
                dve.tensor_tensor(em[:, :, :], e8[:, :, :], mask[:, :, :], ALU.mult).then_inc(s_em, 1)
                dve.wait_ge(s_em, C + 1)
                dve.tensor_reduce(gsum[:, :], em[:, :, :], AX.X, ALU.add).then_inc(s_gs, 1)
                dve.wait_ge(s_gs, C + 1)
                dve.reciprocal(grcp[:, :], gsum[:, :]).then_inc(s_gr, 1)
                dve.wait_ge(s_gr, C + 1)
                r = grcp[:, :].rearrange("p (u a) -> p u a", a=1)
                dve.tensor_tensor(gpad[:, :, 0:EXPERTS], em[:, :, :], over(r), ALU.mult)
                dve.tensor_tensor(gpad[:, :, 32:32 + EXPERTS], em[:, :, :], over(r),
                                  ALU.mult).then_inc(s_g, 1)

            def gate_lo(C, q):
                dve.wait_ge(s_ghi, C + 1)
                rows = slice(32, 32 + EXPERTS)
                low(gT[rows, q, :], mb[rows, 1, :], gT[rows, q, :], s_glo)

            moments(0)
            dve.wait_ge(s_rwhi, 1)
            low(rw1_hl[:, LO, :], rw1_raw[:, :], rw1_hl[:, HI, :], s_rwlo)
            dve.wait_ge(s_b2hi, 1)
            low(b2_hl[:, LO, :], b2_raw[:, :], b2_hl[:, HI, :], s_b2lo)
            normalise(0)
            x_lo(0, 0)
            dve.wait_ge(s_pad, 1)
            dve.wait_ge(s_io, 1)
            top_two(0)
            gates(0)
            gate_lo(0, 0)

            def scale(C, k):
                if k % FT == 0:
                    dve.wait_ge(s_gbc, C * EXPERTS + k // FT + 1)
                dve.wait_ge(s_z, C * SLOTS + k + 1)
                dve.scalar_tensor_tensor(tt[:, k % 4, :], zb[:, k % 4, :], biasT[:, k:k + 1],
                                         gbc[:, k // FT % 2, :], ALU.add, ALU.mult).then_inc(s_tt, 1)

            def hidden_lo(C, k):
                dve.wait_ge(s_hhi, C * SLOTS + k + 1)
                dve.scalar_tensor_tensor(h_hl[:, k % 4, LO, :], tt[:, k % 4, :], 0.0,
                                         h_hl[:, k % 4, HI, :].bitcast(f32), ALU.max,
                                         ALU.subtract).then_inc(s_hlo, 1)

            def add_y(C):
                dve.wait_ge(s_yt, C + 1)
                tok = x_sb[:, ds(C * TPC, TPC), :].rearrange("p u d -> p (u d)")
                dve.tensor_tensor(tok, mb[:, 1, :], tok, ALU.add).then_inc(s_yadd, 1)

            def phase(C, p, prep=True, first=False):
                q = 1 - p
                for k in range(SLOTS):
                    scale(C, k)
                    if k > 0:
                        hidden_lo(C, k - 1)
                    elif not first:
                        hidden_lo(C - 1, SLOTS - 1)
                    if k == 4 and not first:
                        add_y(C - 1)
                    if prep:
                        if k == 0:
                            moments(C + 1)
                        if k == 3:
                            normalise(C + 1)
                        if k == AT_XT + 1:
                            x_lo(C + 1, q)
                        if k == AT_ST + 1:
                            top_two(C + 1)
                        if k == AT_ST + 4:
                            gates(C + 1)
                        if k == AT_GT + 2:
                            gate_lo(C + 1, q)

            phase(0, 0, first=True)
            with dve.Fori(0, (CHUNKS - 2) // 2) as i:
                phase(i * 2 + 1, 1)
                phase(i * 2 + 2, 0)
            phase(CHUNKS - 1, 1, prep=False)
            hidden_lo(CHUNKS - 1, SLOTS - 1)
            add_y(CHUNKS - 1)

        @block.tensor
        def _(pe):
            def product(out, lhs, rhs, start, stop):
                pe.matmul(out, lhs(HI), rhs(HI), start=start, stop=False)
                pe.matmul(out, lhs(HI), rhs(LO), start=False, stop=False)
                return pe.matmul(out, lhs(LO), rhs(HI), start=False, stop=stop)

            pe.transpose(gb[:, 0:NB], bias_raw[:, :], ident[0:NB, 0:NB]).then_inc(s_bt, 1)

            def x_transposes(C):
                pe.wait_ge(s_xn, C + 1)
                for u in range(TPC):
                    last = pe.transpose(mb[:, 0, u * P:(u + 1) * P], xn[:, u * D:(u + 1) * D], ident[:, :])
                last.then_inc(s_xt, 1)

            def router(C, q, f):
                if f == 0:
                    pe.wait_ge(s_xlo, C + 1)
                else:
                    if f >= 2:
                        pe.wait_ge(s_rh, C * FT + f - 1)
                product(mb[:, (f + 1) % 2, :], lambda a: rw1_hl[:, a, f * P:(f + 1) * P],
                        lambda a: xT_hl[:, q, a, :], True, True).then_inc(s_r, 1)

            def score(C):
                pe.wait_ge(s_rh, (C + 1) * FT)
                for f in range(FT):
                    last = pe.matmul(mb[0:EXPERTS, 1, :], rw2[:, f, :], rh[:, f, :],
                                     start=f == 0, stop=f == FT - 1)
                last.then_inc(s_s, 1)

            def score_transposes(C):
                pe.wait_ge(s_sT, C + 1)
                pe.sem_inc(s_pass, 1)
                for u in range(TPC):
                    last = pe.transpose(mb[:, 0, u * EXPERTS:(u + 1) * EXPERTS],
                                        sT[:, u * P:(u + 1) * P], ident[0:EXPERTS, 0:EXPERTS])
                last.then_inc(s_st, 1)

            def gate_transposes(C):
                pe.wait_ge(s_g, C + 1)
                for u in range(TPC):
                    last = pe.transpose(mb[:, 1, u * P:(u + 1) * P], gpad[:, u, :], ident[:, :])
                last.then_inc(s_gt, 1)

            def spread(C, p, e):
                if e == 0:
                    pe.wait_ge(s_glo, C + 1)
                else:
                    pe.wait_ge(s_gbc, C * EXPERTS + e)
                pe.matmul(gb[:, :], sel[:, e, :], gT[:, p, :], start=True, stop=True).then_inc(s_gb, 1)

            def first_product(C, p, k, first):
                if k % FT == 0 and first:
                    pe.wait_ge(s_w1lo, k // FT + 1)
                if not (first and k < 4):
                    pe.wait_ge(s_tt, C * SLOTS + k - 3)
                product(zb[:, k % 4, :], lambda a: w1_hl[:, a, k // FT, k % FT * P:(k % FT + 1) * P],
                        lambda a: xT_hl[:, p, a, :], True, True).then_inc(s_z, 1)

            def second_product(C, k, first):
                if k % FT == 0 and first:
                    pe.wait_ge(s_w2lo, k // FT + 1)
                if k == 0 and not first:
                    pe.wait_ge(s_ysb, C)
                pe.wait_ge(s_hlo, C * SLOTS + k + 1)
                product(yb[:, :], lambda a: w2_hl[:, a, k // FT, k % FT * D:(k % FT + 1) * D],
                        lambda a: h_hl[:, k % 4, a, :], k == 0, False).then_inc(s_w2, 1)

            def finish(C, p):
                pe.matmul(yb[:, :], b2_hl[:, HI, :], gT[:, p, :], start=False, stop=False)
                pe.matmul(yb[:, :], b2_hl[:, LO, :], gT[:, p, :], start=False, stop=True).then_inc(s_y, 1)

            def y_transposes(C):
                pe.wait_ge(s_ysb, C + 1)
                for u in range(TPC):
                    last = pe.transpose(mb[:, 1, u * P:(u + 1) * P], y_sb[:, u * P:(u + 1) * P], ident[:, :])
                last.then_inc(s_yt, 1)

            def phase(C, p, prep=True, first=False):
                q = 1 - p
                for k in range(SLOTS):
                    first_product(C, p, k, first)
                    if k % FT == 1 and k + FT < SLOTS:
                        spread(C, p, k // FT + 1)
                    if k >= LAG:
                        second_product(C, k - LAG, first)
                    elif not first:
                        second_product(C - 1, SLOTS - LAG + k, False)
                        if k == LAG - 1:
                            finish(C - 1, q)
                    if k == 4 and not first:
                        y_transposes(C - 1)
                    if prep:
                        if k == AT_XT:
                            x_transposes(C + 1)
                        for f in range(FT):
                            if k == AT_R[f]:
                                if f == 0 and not first:
                                    pe.wait_ge(s_yadd, C)
                                router(C + 1, q, f)
                        if k == AT_S:
                            score(C + 1)
                        if k == AT_ST:
                            score_transposes(C + 1)
                        if k == AT_GT:
                            gate_transposes(C + 1)
                        if k == SLOTS - 1:
                            spread(C + 1, q, 0)

            x_transposes(0)
            pe.wait_ge(s_rwlo, 1)
            for f in range(FT):
                router(0, 0, f)
            score(0)
            score_transposes(0)
            gate_transposes(0)
            pe.wait_ge(s_sel, 1)
            pe.wait_ge(s_bias, 1)
            pe.wait_ge(s_b2lo, 1)
            spread(0, 0, 0)
            phase(0, 0, first=True)
            with pe.Fori(0, (CHUNKS - 2) // 2) as i:
                phase(i * 2 + 1, 1)
                phase(i * 2 + 2, 0)
            phase(CHUNKS - 1, 1, prep=False)
            for k in range(SLOTS - LAG, SLOTS):
                second_product(CHUNKS - 1, k, False)
            finish(CHUNKS - 1, 1)
            y_transposes(CHUNKS - 1)


def build(nc, t):
    from concourse import mybir
    from contextlib import ExitStack

    f32 = mybir.dt.float32
    with ExitStack() as ctx:
        t["x_sb"] = ctx.enter_context(nc.sbuf_tensor("x_sb", [P, TILES, D], f32))
        t["ident"] = ctx.enter_context(nc.sbuf_tensor("ident", [P, P], f32))
        for name, shape in (("w1_raw", [P, EXPERTS, FF]), ("rw1_raw", [P, FF]), ("rw2_sb", [P, FT, EXPERTS]),
                            ("bias_raw", [(EXPERTS + 1) * FT, P]), ("rb2_sb", [EXPERTS, 1]),
                            ("b2_raw", [GR, D])):
            t[name] = ctx.enter_context(nc.sbuf_tensor(name, shape, f32))
        attention(nc, t)
        experts(nc, t)


_INS = {"L0_attn_x": "x", "L0_attn_proj_q": "wq", "L0_attn_proj_k": "wk", "L0_attn_proj_v": "wv",
        "L0_attn_proj_o": "wo", "L0_ffn_rw1": "rw1", "L0_ffn_rb1": "rb1", "L0_ffn_rw2": "rw2",
        "L0_ffn_rb2": "rb2", "L0_ffn_W1": "W1", "L0_ffn_b1": "b1", "L0_ffn_W2": "W2", "L0_ffn_b2": "b2"}


def kernel(**inputs):
    import concourse.bacc as bacc
    from concourse import mybir
    from concourse.bass_utils import run_bass_kernel_spmd as run

    nc = bacc.Bacc("TRN2", target_bir_lowering=False, num_devices=1)
    arrays, t = {}, {}
    for name, short in _INS.items():
        a = np.ascontiguousarray(inputs[name])
        arrays[name] = a
        t[short] = nc.dram_tensor(name, a.shape, mybir.dt.from_np(a.dtype), kind="ExternalInput").ap()
    t["out"] = nc.dram_tensor("out", (B, N, D), mybir.dt.float32, kind="ExternalOutput").ap()
    build(nc, t)
    return run(nc, [arrays], core_ids=[0]).results[0]["out"]
```

```python
import numpy as np

B, N, D = 2, 2048, 128
HEADS = 8
P = 128
EPS = 1e-5
FF = 512
EXPERTS = 8
CH = 512
TPC = CH // P
TPB = N // P
CPB = N // CH
GPB = CPB * HEADS
TILES = B * TPB
CHUNKS = B * CPB
FT = FF // P
HI, LO = 0, 1
GR = 64


def attention(nc, t):
    import concourse.bass as bass
    from concourse import mybir
    from contextlib import ExitStack

    f32, f32r = mybir.dt.float32, mybir.dt.float32r
    ALU, ACT, AX = mybir.AluOpType, mybir.ActivationFunctionType, mybir.AxisListType
    ds = bass.ds
    x_sb, ident = t["x_sb"], t["ident"]
    SP = 96
    YW = D + 2
    AHEAD = 3
    PV_LAG = 3
    AT_COPY, AT_O, AT_Y, AT_G, AT_MAX = 4, 3, 6, 10, 14

    with ExitStack() as ctx:
        def sb(name, shape, dt=f32):
            return ctx.enter_context(nc.sbuf_tensor(name, shape, dt))

        def pb(name, shape):
            return ctx.enter_context(nc.psum_tensor(name, shape, f32))

        def sem(name):
            return ctx.enter_context(nc.semaphore(name))

        wq_raw = sb("wq_raw", [P, HEADS, D])
        wo_raw = sb("wo_raw", [P, HEADS, D])
        wkv_raw = sb("wkv_raw", [P, 2, D])
        lhs_f = sb("lhs_f", [P, HEADS, D])
        lhs_hl = sb("lhs_hl", [P, 2, HEADS, D], f32r)
        kv_f = sb("kv_f", [P, 2, D])
        kv_hl = sb("kv_hl", [P, 2, 2, D], f32r)
        woT_hl = sb("woT_hl", [P, 2, HEADS, D], f32r)
        a_hl = sb("a_hl", [P, HEADS, 2, D], f32r)
        a_cur = sb("a_cur", [P, 2, 2, D], f32r)
        m_hl = sb("m_hl", [P, 2, HEADS, YW], f32r)
        bn = sb("bn", [P, TPB, 6])
        mv = sb("mv", [P, TPB, 2])
        mhalf = sb("mhalf", [P, TPB])
        rstd = sb("rstd", [P, TPB])
        xn = sb("xn", [P, TPB, D])
        val_hl = sb("val_hl", [P, 2, TPB, D], f32r)
        key_hl = sb("key_hl", [P, 2, N], f32r)
        new_hi = sb("new_hi", [P, 2, CH], f32r)
        new_lo = sb("new_lo", [P, CH], f32r)
        q_hl = sb("q_hl", [P, 2, 2, CH], f32r)
        mx = sb("mx", [P, 2, TPC, CPB])
        pad = sb("pad", [P, TPC, P])
        pf = sb("pf", [P, 4, CH])
        pt_hl = sb("pt_hl", [P, 4, 2, CH], f32r)
        oT_hl = sb("oT_hl", [P, 2, CH], f32r)
        rcp = sb("rcp", [P, TPC])

        st = pb("st", [P, 2, CH])
        mp = pb("mp", [P, 2, CH])
        ob = pb("ob", [P, 2, CH])
        wb = pb("wb", [P, 2, CH])

        s_x, s_w = sem("x_loaded"), sem("w_loaded")
        s_b2c, s_ffn = sem("b2_cleared"), sem("ffn_loaded")
        s_id0, s_id = sem("ident_cleared"), sem("ident_ready")
        s_mh, s_pad, s_pick = sem("mhalf_ready"), sem("pad_cleared"), sem("m_pick_ready")
        s_pass = sem("passed")
        s_wt, s_wf = sem("weights_transposed"), sem("weights_reduced")
        s_whi, s_wlo = sem("weights_hi"), sem("weights_lo")
        s_am, s_amhi, s_amlo = sem("folded"), sem("folded_hi"), sem("folded_lo")
        s_bn, s_mv, s_ve = sem("bn_stats"), sem("mean_var"), sem("var_eps")
        s_rstd, s_xn, s_one = sem("rstd_ready"), sem("xn_ready"), sem("xn_one")
        s_vhi, s_vlo = sem("val_hi"), sem("val_lo")
        s_xt, s_xhi, s_xlo = sem("xn_transposed"), sem("xT_hi"), sem("xT_lo")
        s_ac = sem("a_copied")
        s_q, s_nhi, s_nlo = sem("queries_done"), sem("new_hi_ready"), sem("new_lo_ready")
        s_chi, s_clo = sem("q_hi_copied"), sem("q_lo_copied")
        s_mp, s_mx, s_nm = sem("max_scores"), sem("tile_max"), sem("row_max")
        s_mt, s_row = sem("max_transposed"), sem("shift_in_q")
        s_st, s_hi, s_lo = sem("scores_done"), sem("exp_hi"), sem("exp_lo")
        s_pv, s_ohi, s_olo = sem("pv_done"), sem("o_hi"), sem("o_lo")
        s_y, s_rcp, s_yadd = sem("y_done"), sem("rcp_ready"), sem("y_added")

        block = ctx.enter_context(nc.Block())

        @block.sync
        def _(sp):
            for b in range(B):
                if b > 0:
                    sp.wait_ge(s_x, 16 * b)
                sp.dma_start(x_sb[:, b * TPB:(b + 1) * TPB, :],
                             t["x"][b, :, :].rearrange("(n p) d -> p n d", p=P)).then_inc(s_x, 16)
            sp.dma_start(t["rw1_raw"][:, :], t["rw1"]).then_inc(s_ffn, 16)
            sp.dma_start(t["rw2_sb"][:, :, :], t["rw2"].rearrange("(f p) e -> p f e", p=P)).then_inc(s_ffn, 16)
            sp.dma_start(t["bias_raw"][0:EXPERTS * FT, :],
                         t["b1"].rearrange("e (f p) -> (e f) p", p=P)).then_inc(s_ffn, 16)
            sp.dma_start(t["bias_raw"][EXPERTS * FT:(EXPERTS + 1) * FT, :],
                         t["rb1"].rearrange("(f p) -> f p", p=P)).then_inc(s_ffn, 16)
            sp.dma_start(t["rb2_sb"][:, :], t["rb2"].rearrange("(e a) -> e a", a=1)).then_inc(s_ffn, 16)
            sp.wait_ge(s_b2c, 1)
            for row in (0, GR // 2):
                sp.dma_start(t["b2_raw"][row:row + EXPERTS, :], t["b2"]).then_inc(s_ffn, 16)
            sp.dma_start(t["w1_raw"][:, :, :], t["W1"].rearrange("e d f -> d e f")).then_inc(s_ffn, 16)
            sp.dma_start(t["w2_raw"][:, :, :].rearrange("p e (f d) -> p (e f) d", f=FT),
                         t["W2"].rearrange("e (f p) d -> p (e f) d", p=P)).then_inc(s_ffn, 16)
            sp.wait_ge(s_ffn, 9 * 16)

        @block.gpsimd
        def _(pool):
            pool.memset(ident[:, :], 0.0).then_inc(s_id0, 1)
            pool.memset(mhalf[:, :], -0.5).then_inc(s_mh, 1)
            pool.memset(t["b2_raw"][:, :], 0.0).then_inc(s_b2c, 1)
            pool.wait_ge(s_id0, 1)
            pool.affine_select(out=ident[:, :], in_=ident[:, :], compare_op=ALU.not_equal, fill=1.0,
                               base=0, pattern=[[-1, P]], channel_multiplier=1).then_inc(s_id, 1)
            pool.memset(pad[:, :, :], 0.0).then_inc(s_pad, 1)
            pool.memset(m_hl[:, :, :, D:YW].bitcast(f32), 0.0).then_inc(s_pick, 1)
            pool.wait_ge(s_mh, 1)

            def copy_a(head, parity):
                pool.tensor_copy(a_cur[:, parity, :, :].rearrange("p a n -> p (a n)"),
                                 a_hl[:, ds(head, 1), :, :].bitcast(f32)
                                 .rearrange("p h a n -> p (h a n)")).then_inc(s_ac, 1)

            def phase(G, head, parity):
                pool.wait_ge(s_q, G + 1)
                pool.sem_inc(s_pass, 1)
                copy_a(head, parity)

            with pool.Fori(0, B) as b:
                pool.wait_ge(s_ve, b + 1)
                pool.tensor_tensor(rstd[:, :], mv[:, :, 1], mhalf[:, :], ALU.pow).then_inc(s_rstd, 1)
                pool.wait_ge(s_amhi, 1)
                pool.wait_ge(s_amlo, 1)
                copy_a(0, 0)
                copy_a(1, 1)
                phase(b * GPB, 2, 0)
                with pool.Fori(0, (GPB - 4) // 2) as i:
                    phase(b * GPB + i * 2 + 1, (i * 2 + 3) & (HEADS - 1), 1)
                    phase(b * GPB + i * 2 + 2, (i * 2 + 4) & (HEADS - 1), 0)
                phase(b * GPB + GPB - 3, HEADS - 1, 1)
                pool.wait_ge(s_q, (b + 1) * GPB)

        @block.scalar
        def _(act):
            act.dma_start(wkv_raw[:, 0, :], t["wk"]).then_inc(s_w, 16)
            act.dma_start(wkv_raw[:, 1, :], t["wv"]).then_inc(s_w, 16)
            act.dma_start(wq_raw[:, :, :], t["wq"].rearrange("h d k -> d h k")).then_inc(s_w, 16)
            act.dma_start(wo_raw[:, :, :], t["wo"].rearrange("h d v -> d h v")).then_inc(s_w, 16)
            act.wait_ge(s_wf, 1)
            act.activation(lhs_hl[:, HI, :, :], lhs_f[:, :, :], ACT.Copy)
            act.activation(kv_hl[:, HI, :, :], kv_f[:, :, :], ACT.Copy)
            act.activation(woT_hl[:, HI, :, :], mp[:, :, :].rearrange("p c (h d) -> p (c h) d", d=D),
                           ACT.Copy).then_inc(s_whi, 1)
            act.wait_ge(s_am, 1)
            act.activation(a_hl[:, :, HI, :], st[:, :, :].rearrange("p c (h d) -> p (c h) d", d=D),
                           ACT.Copy)
            act.activation(m_hl[:, HI, :, 0:D], ob[:, :, :].rearrange("p c (h d) -> p (c h) d", d=D),
                           ACT.Copy).then_inc(s_amhi, 1)

            def xt_hi(b, c):
                act.wait_ge(s_xt, b * CPB + c + 1)
                act.activation(key_hl[:, HI, c * CH:(c + 1) * CH], wb[:, c % 2, :],
                               ACT.Copy).then_inc(s_xhi, 1)

            def new_queries_hi(G, k):
                act.wait_ge(s_q, G + 1)
                act.activation(new_hi[:, k % 2, :], wb[:, 0, :], ACT.Copy).then_inc(s_nhi, 1)

            def copy_q_hi(G, k):
                act.wait_ge(s_nhi, G + 1)
                act.activation(q_hl[:, k % 2, HI, :], new_hi[:, k % 2, :].bitcast(f32),
                               ACT.Copy).then_inc(s_chi, 1)

            def shift_row(G, k):
                act.wait_ge(s_mt, G + 1)
                act.activation(q_hl[SP:SP + 1, k % 2, HI, :], wb[SP:SP + 1, 1, :],
                               ACT.Copy).then_inc(s_row, 1)

            def exps(G, tile, fresh=False):
                act.wait_ge(s_st, G * TPB + tile + 1)
                if not fresh:
                    act.wait_ge(s_pv, G * TPB + tile - 3)
                act.activation(pf[:, tile % 4, :], st[:, tile % 2, :], ACT.Exp)
                act.activation(pt_hl[:, tile % 4, HI, :], st[:, tile % 2, :], ACT.Exp).then_inc(s_hi, 1)

            def o_hi(G, p):
                act.wait_ge(s_pv, (G + 1) * TPB)
                act.activation(oT_hl[:, HI, :], ob[:, p, :], ACT.Copy).then_inc(s_ohi, 1)

            def phase(G, p, first=False, following=True, queries=True):
                q = 1 - p
                for s in range(TPB):
                    exps(G, s, fresh=first and s < 4)
                    if s == AT_O and not first:
                        o_hi(G - 1, q)
                    if s == AT_COPY and following:
                        copy_q_hi(G + 1, q)
                    if s == AT_G and queries:
                        new_queries_hi(G + 2, p)
                    if s == AT_MAX and following:
                        shift_row(G + 1, q)

            with act.Fori(0, B) as b:
                for c in range(CPB):
                    act.wait_ge(s_one, b * CPB + c + 1)
                    act.activation(val_hl[:, HI, c * TPC:(c + 1) * TPC, :],
                                   xn[:, c * TPC:(c + 1) * TPC, :], ACT.Copy).then_inc(s_vhi, 1)
                    xt_hi(b, c)
                new_queries_hi(b * GPB, 0)
                copy_q_hi(b * GPB, 0)
                new_queries_hi(b * GPB + 1, 1)
                shift_row(b * GPB, 0)
                phase(b * GPB, 0, first=True)
                with act.Fori(0, (GPB - 4) // 2) as i:
                    phase(b * GPB + i * 2 + 1, 1)
                    phase(b * GPB + i * 2 + 2, 0)
                phase(b * GPB + GPB - 3, 1)
                phase(b * GPB + GPB - 2, 0, queries=False)
                phase(b * GPB + GPB - 1, 1, following=False, queries=False)
                o_hi(b * GPB + GPB - 1, 1)

        @block.vector
        def _(dve):
            def low(out, x, hi):
                return dve.tensor_tensor(out, x, hi.bitcast(f32), ALU.subtract)

            dve.wait_ge(s_pick, 1)
            dve.memset(m_hl[SP:SP + 1, HI, :, D:D + 1].bitcast(f32), 1.0).then_inc(s_pick, 1)
            dve.wait_ge(s_wt, 1)
            for h in range(HEADS):
                src = st[:, h // TPC, h % TPC * D:(h % TPC + 1) * D]
                dve.tensor_scalar(lhs_f[:, h, :], src, src[:, SP:SP + 1], None, ALU.subtract)
            for n in range(2):
                src = wb[:, 0, n * D:(n + 1) * D]
                last = dve.tensor_scalar(kv_f[:, n, :], src, src[:, SP:SP + 1], None, ALU.subtract)
            last.then_inc(s_wf, 1)
            dve.wait_ge(s_whi, 1)
            low(lhs_hl[:, LO, :, :], lhs_f[:, :, :], lhs_hl[:, HI, :, :])
            low(kv_hl[:, LO, :, :], kv_f[:, :, :], kv_hl[:, HI, :, :])
            low(woT_hl[:, LO, :, :], mp[:, :, :].rearrange("p c (h d) -> p (c h) d", d=D),
                woT_hl[:, HI, :, :]).then_inc(s_wlo, 1)
            dve.wait_ge(s_amhi, 1)
            low(a_hl[:, :, LO, :], st[:, :, :].rearrange("p c (h d) -> p (c h) d", d=D), a_hl[:, :, HI, :])
            low(m_hl[:, LO, :, 0:D], ob[:, :, :].rearrange("p c (h d) -> p (c h) d", d=D),
                m_hl[:, HI, :, 0:D]).then_inc(s_amlo, 1)
            dve.wait_ge(s_pad, 1)

            def new_queries_lo(G, k):
                dve.wait_ge(s_nhi, G + 1)
                low(new_lo[:, :], wb[:, 0, :], new_hi[:, k % 2, :]).then_inc(s_nlo, 1)

            def copy_q_lo(G, k):
                dve.wait_ge(s_nlo, G + 1)
                dve.tensor_copy(q_hl[:, k % 2, LO, :], new_lo[:, :].bitcast(f32)).then_inc(s_clo, 1)

            def tile_max(G, k, n):
                dve.wait_ge(s_mp, G * TPB + n + 1)
                dve.tensor_reduce(mx[:, k, n // CPB, n % CPB:n % CPB + 1], mp[:, n % 2, :], AX.X,
                                  ALU.max).then_inc(s_mx, 1)

            def row_max(G, k):
                dve.wait_ge(s_mx, (G + 1) * TPB)
                dve.tensor_reduce(pad[:, :, SP], mx[:, k, :, :], AX.X, ALU.max,
                                  negate=True).then_inc(s_nm, 1)

            def exp_lo(G, tile):
                dve.wait_ge(s_hi, G * TPB + tile + 1)
                low(pt_hl[:, tile % 4, LO, :], pf[:, tile % 4, :], pt_hl[:, tile % 4, HI, :])\
                    .then_inc(s_lo, 1)

            def o_lo(G, p):
                dve.wait_ge(s_ohi, G + 1)
                low(oT_hl[:, LO, :], ob[:, p, :], oT_hl[:, HI, :]).then_inc(s_olo, 1)

            def y_add(G, tile0):
                dve.wait_ge(s_y, G + 1)
                units = wb[:, :, 0:2 * YW].rearrange("p c (u w) -> p c u w", w=YW)
                dve.reciprocal(rcp[:, :].rearrange("p (c u) -> p c u", u=2),
                               units[:, :, :, D]).then_inc(s_rcp, 1)
                dve.wait_ge(s_rcp, G + 1)
                for u in range(TPC):
                    tok = x_sb[:, ds(tile0 + u, 1), :].rearrange("p a d -> p (a d)")
                    last = dve.scalar_tensor_tensor(tok, units[:, u // 2, u % 2, 0:D],
                                                    rcp[:, u:u + 1], tok, ALU.mult, ALU.add)
                last.then_inc(s_yadd, 1)

            def phase(G, p, tile0, first=False, following=True, queries=True):
                q = 1 - p
                for s in range(TPB):
                    n = s + AHEAD
                    if n < TPB and following:
                        tile_max(G + 1, q, n)
                    elif n >= TPB and queries:
                        tile_max(G + 2, p, n - TPB)
                    if s > 0:
                        exp_lo(G, s - 1)
                    elif not first:
                        exp_lo(G - 1, TPB - 1)
                    if n == TPB - 1 and following:
                        row_max(G + 1, q)
                    if s == AT_O and not first:
                        o_lo(G - 1, q)
                    if s == AT_COPY and following:
                        copy_q_lo(G + 1, q)
                    if s == AT_Y and not first:
                        y_add(G - 1, tile0)
                    if s == AT_G and queries:
                        new_queries_lo(G + 2, p)

            with dve.Fori(0, B) as b:
                dve.wait_ge(s_x, b * 16 + 16)
                for n in range(TPB):
                    last = dve.bn_stats(bn[:, n, :], x_sb[:, ds(b * TPB + n, 1), :]
                                        .rearrange("p a d -> p (a d)"))
                last.then_inc(s_bn, 1)
                dve.wait_ge(s_bn, b + 1)
                dve.sem_inc(s_pass, 1)
                for n in range(TPB):
                    last = dve.bn_aggr(mv[:, n, :], bn[:, n, :])
                last.then_inc(s_mv, 1)
                dve.wait_ge(s_mv, b + 1)
                dve.tensor_scalar(mv[:, :, 1], mv[:, :, 1], EPS, None, ALU.add).then_inc(s_ve, 1)
                dve.wait_ge(s_rstd, b + 1)
                for c in range(CPB):
                    for n in range(c * TPC, (c + 1) * TPC):
                        last = dve.tensor_scalar(xn[:, n, :], x_sb[:, ds(b * TPB + n, 1), :]
                                                 .rearrange("p a d -> p (a d)"),
                                                 mv[:, n, 0:1], rstd[:, n:n + 1], ALU.subtract, ALU.mult)
                    last.then_inc(s_xn, 1)
                    dve.wait_ge(s_xn, b * CPB + c + 1)
                    dve.memset(xn[:, c * TPC:(c + 1) * TPC, SP:SP + 1], 1.0).then_inc(s_one, 1)
                for c in range(CPB):
                    dve.wait_ge(s_vhi, b * CPB + c + 1)
                    low(val_hl[:, LO, c * TPC:(c + 1) * TPC, :], xn[:, c * TPC:(c + 1) * TPC, :],
                        val_hl[:, HI, c * TPC:(c + 1) * TPC, :]).then_inc(s_vlo, 1)
                    dve.wait_ge(s_xhi, b * CPB + c + 1)
                    low(key_hl[:, LO, c * CH:(c + 1) * CH], wb[:, c % 2, :],
                        key_hl[:, HI, c * CH:(c + 1) * CH]).then_inc(s_xlo, 1)
                new_queries_lo(b * GPB, 0)
                copy_q_lo(b * GPB, 0)
                dve.wait_ge(s_clo, b * GPB + 1)
                new_queries_lo(b * GPB + 1, 1)
                for n in range(TPB):
                    tile_max(b * GPB, 0, n)
                row_max(b * GPB, 0)
                for n in range(AHEAD):
                    tile_max(b * GPB + 1, 1, n)
                T0 = b * TPB
                last_chunk = TPB - TPC
                phase(b * GPB, 0, None, first=True)
                with dve.Fori(0, (GPB - 4) // 2) as i:
                    phase(b * GPB + i * 2 + 1, 1, T0 + (i & last_chunk))
                    phase(b * GPB + i * 2 + 2, 0, T0 + (i & last_chunk))
                phase(b * GPB + GPB - 3, 1, T0 + last_chunk)
                phase(b * GPB + GPB - 2, 0, T0 + last_chunk, queries=False)
                phase(b * GPB + GPB - 1, 1, T0 + last_chunk, following=False, queries=False)
                exp_lo(b * GPB + GPB - 1, TPB - 1)
                o_lo(b * GPB + GPB - 1, 1)
                y_add(b * GPB + GPB - 1, T0 + last_chunk)

        @block.tensor
        def _(pe):
            def product(out, lhs, rhs, start, stop):
                pe.matmul(out, lhs(HI), rhs(HI), start=start, stop=False)
                pe.matmul(out, lhs(HI), rhs(LO), start=False, stop=False)
                return pe.matmul(out, lhs(LO), rhs(HI), start=False, stop=stop)

            pe.wait_ge(s_id, 1)
            pe.wait_ge(s_w, 64)
            for h in range(HEADS):
                cols = slice(h % TPC * D, (h % TPC + 1) * D)
                pe.transpose(st[:, h // TPC, cols], wq_raw[:, h, :], ident[:, :])
                pe.transpose(mp[:, h // TPC, cols], wo_raw[:, h, :], ident[:, :])
            for n in range(2):
                last = pe.transpose(wb[:, 0, n * D:(n + 1) * D], wkv_raw[:, n, :], ident[:, :])
            last.then_inc(s_wt, 1)
            pe.wait_ge(s_wlo, 1)
            for h in range(HEADS):
                cols = slice(h % TPC * D, (h % TPC + 1) * D)
                product(st[:, h // TPC, cols], lambda a: lhs_hl[:, a, h, :], lambda a: kv_hl[:, a, 0, :],
                        True, True)
                last = product(ob[:, h // TPC, cols], lambda a: kv_hl[:, a, 1, :],
                               lambda a: woT_hl[:, a, h, :], True, True)
            last.then_inc(s_am, 1)
            pe.wait_ge(s_amlo, 1)
            pe.wait_ge(s_pick, 2)

            def queries(G, k, col):
                pe.wait_ge(s_ac, G + 1)
                product(wb[:, 0, :], lambda a: a_cur[:, k % 2, a, :],
                        lambda a: key_hl[:, a, ds(col, CH)], True, True).then_inc(s_q, 1)

            def max_scores(G, k, n, fresh=False):
                if n == 0:
                    pe.wait_ge(s_nhi, G + 1)
                if not (fresh and n < 2):
                    pe.wait_ge(s_mx, G * TPB + n - 1)
                unit, c = n // CPB, n % CPB
                pe.matmul(mp[:, n % 2, :], new_hi[:, k % 2, unit * P:(unit + 1) * P],
                          key_hl[:, HI, c * CH:(c + 1) * CH], start=True, stop=True).then_inc(s_mp, 1)

            def max_transposes(G):
                pe.wait_ge(s_nm, G + 1)
                for u in range(TPC):
                    last = pe.transpose(wb[:, 1, u * P:(u + 1) * P], pad[:, u, :], ident[:, :])
                last.then_inc(s_mt, 1)

            def scores(G, p, tile, fresh=False):
                if tile == 0:
                    pe.wait_ge(s_clo, G + 1)
                    pe.wait_ge(s_row, G + 1)
                if not fresh:
                    pe.wait_ge(s_hi, G * TPB + tile - 1)
                product(st[:, tile % 2, :], lambda a: key_hl[:, a, tile * P:(tile + 1) * P],
                        lambda a: q_hl[:, p, a, :], True, True).then_inc(s_st, 1)

            def pv(G, p, tile):
                pe.wait_ge(s_lo, G * TPB + tile + 1)
                product(ob[:, p, :], lambda a: val_hl[:, a, tile, :],
                        lambda a: pt_hl[:, tile % 4, a, :],
                        tile == 0, tile == TPB - 1).then_inc(s_pv, 1)

            def project(G, head):
                pe.wait_ge(s_olo, G + 1)
                for u in range(TPC):
                    last = product(wb[:, u // 2, u % 2 * YW:(u % 2 + 1) * YW],
                                   lambda a: oT_hl[:, a, u * P:(u + 1) * P],
                                   lambda a: m_hl[:, a, ds(head, 1), :].rearrange("p h w -> p (h w)"),
                                   True, True)
                last.then_inc(s_y, 1)

            def phase(G, p, head, col, first=False, following=True, queries_=True):
                q = 1 - p
                for s in range(TPB):
                    scores(G, p, s, fresh=first and s < 2)
                    n = s + AHEAD
                    if n < TPB and following:
                        max_scores(G + 1, q, n)
                    elif n >= TPB and queries_:
                        max_scores(G + 2, p, n - TPB)
                    if s >= PV_LAG:
                        pv(G, p, s - PV_LAG)
                    elif not first:
                        pv(G - 1, q, TPB - PV_LAG + s)
                    if s == AT_Y and not first:
                        if following:
                            pe.wait_ge(s_nlo, G + 2)
                        project(G - 1, head)
                    if s == AT_G and queries_:
                        if not first:
                            pe.wait_ge(s_yadd, G)
                        queries(G + 2, p, col)
                    if s == AT_MAX and following:
                        if not first and not queries_:
                            pe.wait_ge(s_yadd, G)
                        max_transposes(G + 1)

            with pe.Fori(0, B) as b:
                for c in range(CPB):
                    pe.wait_ge(s_one, b * CPB + c + 1)
                    if c >= 2:
                        pe.wait_ge(s_xlo, b * CPB + c - 1)
                    for u in range(TPC):
                        last = pe.transpose(wb[:, c % 2, u * P:(u + 1) * P], xn[:, c * TPC + u, :],
                                            ident[:, :])
                    last.then_inc(s_xt, 1)
                pe.wait_ge(s_xlo, (b + 1) * CPB)
                queries(b * GPB, 0, 0)
                pe.wait_ge(s_nlo, b * GPB + 1)
                queries(b * GPB + 1, 1, 0)
                for n in range(TPB):
                    max_scores(b * GPB, 0, n, fresh=True)
                max_scores(b * GPB + 1, 1, 0)
                max_scores(b * GPB + 1, 1, 1)
                max_scores(b * GPB + 1, 1, 2)
                pe.wait_ge(s_vlo, (b + 1) * CPB)
                max_transposes(b * GPB)
                phase(b * GPB, 0, None, 0, first=True)
                with pe.Fori(0, (GPB - 4) // 2) as i:
                    phase(b * GPB + i * 2 + 1, 1, (i * 2) & (HEADS - 1), ((i + 1) & (TPB - TPC)) * P)
                    phase(b * GPB + i * 2 + 2, 0, (i * 2 + 1) & (HEADS - 1), ((i + 2) & (TPB - TPC)) * P)
                phase(b * GPB + GPB - 3, 1, HEADS - 4, N - CH)
                phase(b * GPB + GPB - 2, 0, HEADS - 3, None, queries_=False)
                phase(b * GPB + GPB - 1, 1, HEADS - 2, None, following=False, queries_=False)
                for tile in range(TPB - PV_LAG, TPB):
                    pv(b * GPB + GPB - 1, 1, tile)
                project(b * GPB + GPB - 1, HEADS - 1)


def experts(nc, t):
    import concourse.bass as bass
    from concourse import mybir
    from contextlib import ExitStack

    f32, f32r, u32 = mybir.dt.float32, mybir.dt.float32r, mybir.dt.uint32
    ALU, ACT, AX = mybir.AluOpType, mybir.ActivationFunctionType, mybir.AxisListType
    ds = bass.ds
    x_sb, ident = t["x_sb"], t["ident"]
    w1_raw, w2_raw, rw1_raw, rw2, bias_raw, rb2, b2_raw = (t[k] for k in (
        "w1_raw", "w2_raw", "rw1_raw", "rw2_sb", "bias_raw", "rb2_sb", "b2_raw"))
    SLOTS = EXPERTS * FT
    LAG = 3
    NB = (EXPERTS + 1) * FT
    AT_XT, AT_R, AT_S, AT_ST, AT_GT = 6, (9, 10, 12, 13), 16, 18, 25

    with ExitStack() as ctx:
        def sb(name, shape, dt=f32):
            return ctx.enter_context(nc.sbuf_tensor(name, shape, dt))

        def pb(name, shape):
            return ctx.enter_context(nc.psum_tensor(name, shape, f32))

        def sem(name):
            return ctx.enter_context(nc.semaphore(name))

        w1_hl = sb("w1_hl", [P, 2, EXPERTS, FF], f32r)
        w2_hl = sb("w2_hl", [P, 2, EXPERTS, FF], f32r)
        rw1_hl = sb("rw1_hl", [P, 2, FF], f32r)
        b2_hl = sb("b2_hl", [GR, 2, D], f32r)
        biasT = sb("biasT", [P, NB])
        sel_f = sb("sel_f", [GR, EXPERTS, P])
        sel = sb("sel", [GR, EXPERTS, P], f32r)
        iota_u = sb("iota_u", [P, TPC, EXPERTS], mybir.dt.int32)
        iota = sb("iota", [P, TPC, EXPERTS])
        bn = sb("bn2", [P, TPC, 6])
        mv = sb("mv2", [P, TPC, 2])
        mhalf = sb("mhalf2", [P, TPC])
        rstd = sb("rstd2", [P, TPC])
        xn = sb("xn2", [P, CH])
        xT_hl = sb("xT_hl", [P, 2, 2, CH], f32r)
        rh = sb("rh", [P, FT, CH])
        sT = sb("sT", [EXPERTS, CH])
        s8 = sb("s8", [P, TPC, EXPERTS])
        top = sb("top", [P, TPC, 8])
        idx = sb("idx", [P, TPC, 8], u32)
        idxf = sb("idxf", [P, TPC, 8])
        is0 = sb("is0", [P, TPC, EXPERTS])
        is1 = sb("is1", [P, TPC, EXPERTS])
        mask = sb("mask", [P, TPC, EXPERTS])
        shifted = sb("shifted", [P, TPC, EXPERTS])
        e8 = sb("e8", [P, TPC, EXPERTS])
        em = sb("em", [P, TPC, EXPERTS])
        gsum = sb("gsum", [P, TPC])
        grcp = sb("grcp", [P, TPC])
        gpad = sb("gpad", [P, TPC, P])
        gT = sb("gT", [GR, 2, CH], f32r)
        gbc = sb("gbc", [P, 2, CH])
        tt = sb("tt", [P, 4, CH])
        h_hl = sb("h_hl", [P, 4, 2, CH], f32r)
        y_sb = sb("y_sb", [P, CH])

        zb = pb("zb", [P, 4, CH])
        yb = pb("yb", [P, CH])
        gb = pb("gb", [P, CH])
        mb = pb("mb", [P, 2, CH])

        s_pad, s_se0, s_se1, s_sel = sem("gpad_cleared"), sem("sel_cleared"), sem("sel_half"), sem("sel_ready")
        s_iu, s_io, s_mh = sem("iota_made"), sem("iota_ready"), sem("mhalf_ready2")
        s_pass = sem("passed2")
        s_bt, s_bias = sem("bias_transposed"), sem("bias_ready")
        s_rwhi, s_rwlo = sem("rw1_hi"), sem("rw1_lo")
        s_b2hi, s_b2lo = sem("b2_hi"), sem("b2_lo")
        s_w1hi, s_w1lo, s_w2hi, s_w2lo = sem("w1_hi"), sem("w1_lo"), sem("w2_hi"), sem("w2_lo")
        s_bn, s_mv, s_ve, s_rstd, s_xn = (sem(n) for n in (
            "bn_stats2", "mean_var2", "var_eps2", "rstd_ready2", "xn_ready2"))
        s_xt, s_xhi, s_xlo = sem("x_transposed"), sem("xT_hi"), sem("xT_lo")
        s_r, s_rh, s_s, s_sT = sem("router_z"), sem("router_h"), sem("scores_done2"), sem("sT_ready")
        s_st, s_s8, s_top, s_idx, s_idf = (sem(n) for n in (
            "scores_transposed", "scores_ready", "top_ready", "idx_ready", "idxf_ready"))
        s_eq, s_mask, s_sh, s_e8, s_em, s_gs, s_gr, s_g = (sem(n) for n in (
            "equal_ready", "mask_ready", "shifted_ready", "gate_exp", "gate_masked", "gate_sum",
            "gate_rcp", "gates_ready"))
        s_gt, s_ghi, s_glo = sem("gates_transposed"), sem("gT_hi"), sem("gT_lo")
        s_gb, s_gbc = sem("gate_spread"), sem("gbc_ready")
        s_z, s_tt, s_hhi, s_hlo, s_w2 = (sem(n) for n in (
            "z_done", "tt_ready", "h_hi", "h_lo", "second_done"))
        s_y, s_ysb, s_yt, s_yadd = sem("y_chunk"), sem("y_in_sbuf"), sem("y_transposed"), sem("y_added2")
        s_out = sem("out_stored")

        block = ctx.enter_context(nc.Block())

        @block.sync
        def _(sp):
            out = t["out"].rearrange("b n d -> (b n) d")
            with sp.Fori(0, CHUNKS) as c:
                sp.wait_ge(s_yadd, c + 1)
                sp.dma_start(out[ds(c * CH, CH), :].rearrange("(u p) d -> p u d", p=P),
                             x_sb[:, ds(c * TPC, TPC), :]).then_inc(s_out, 16)
            sp.wait_ge(s_out, 16 * CHUNKS)

        @block.gpsimd
        def _(pool):
            pool.memset(mhalf[:, :], -0.5).then_inc(s_mh, 1)
            pool.wait_ge(s_mh, 1)

            def power(c1):
                pool.wait_ge(s_ve, c1)
                pool.tensor_tensor(rstd[:, :], mv[:, :, 1], mhalf[:, :], ALU.pow).then_inc(s_rstd, 1)

            power(1)
            pool.memset(gpad[:, :, :], 0.0).then_inc(s_pad, 1)
            pool.memset(sel_f[:, :, :], 0.0).then_inc(s_se0, 1)
            for half, (before, after) in enumerate(((s_se0, s_se1), (s_se1, s_se1))):
                pool.wait_ge(before, 1)
                pool.affine_select(out=sel_f[:, :, :], in_=sel_f[:, :, :], compare_op=ALU.not_equal,
                                   fill=1.0, base=-32 * half, pattern=[[-1, EXPERTS], [0, P]],
                                   channel_multiplier=1).then_inc(after, 1)
            pool.wait_ge(s_se1, 2)
            pool.tensor_copy(sel[:, :, :], sel_f[:, :, :]).then_inc(s_sel, 1)
            pool.iota(iota_u[:, :, :], pattern=[[0, TPC], [1, EXPERTS]], base=0,
                      channel_multiplier=0).then_inc(s_iu, 1)
            pool.wait_ge(s_iu, 1)
            pool.tensor_copy(iota[:, :, :], iota_u[:, :, :]).then_inc(s_io, 1)
            for raw, hl, hi, lo in ((w1_raw, w1_hl, s_w1hi, s_w1lo), (w2_raw, w2_hl, s_w2hi, s_w2lo)):
                for e in range(EXPERTS):
                    pool.wait_ge(hi, e + 1)
                    pool.tensor_tensor(hl[:, LO, e, :], raw[:, e, :], hl[:, HI, e, :].bitcast(f32),
                                       ALU.subtract).then_inc(lo, 1)
            with pool.Fori(1, CHUNKS) as c:
                power(c + 1)

        @block.scalar
        def _(act):
            act.activation(rw1_hl[:, HI, :], rw1_raw[:, :], ACT.Copy).then_inc(s_rwhi, 1)
            act.activation(b2_hl[:, HI, :], b2_raw[:, :], ACT.Copy).then_inc(s_b2hi, 1)
            act.wait_ge(s_bt, 1)
            act.activation(biasT[:, :], gb[:, 0:NB], ACT.Copy).then_inc(s_bias, 1)
            act.wait_ge(s_bias, 1)

            def x_hi(C, q):
                act.wait_ge(s_xt, C + 1)
                act.activation(xT_hl[:, q, HI, :], mb[:, 0, :], ACT.Copy).then_inc(s_xhi, 1)

            def router_h(C, f):
                act.wait_ge(s_r, C * FT + f + 1)
                act.activation(rh[:, f, :], mb[:, (f + 1) % 2, :], ACT.Relu,
                               bias=biasT[:, EXPERTS * FT + f:EXPERTS * FT + f + 1]).then_inc(s_rh, 1)

            def score(C):
                act.wait_ge(s_s, C + 1)
                act.activation(sT[:, :], mb[0:EXPERTS, 1, :], ACT.Identity, bias=rb2[:, :]).then_inc(s_sT, 1)

            def gate_exp(C):
                act.wait_ge(s_sh, C + 1)
                act.activation(e8[:, :, :], shifted[:, :, :], ACT.Exp).then_inc(s_e8, 1)

            def gate_hi(C, q):
                act.wait_ge(s_gt, C + 1)
                act.activation(gT[:, q, :], mb[0:GR, 1, :], ACT.Copy).then_inc(s_ghi, 1)

            def gate_copy(C, e):
                act.wait_ge(s_gb, C * EXPERTS + e + 1)
                act.activation(gbc[:, e % 2, :], gb[:, :], ACT.Copy).then_inc(s_gbc, 1)

            x_hi(0, 0)
            for e in range(EXPERTS):
                act.activation(w1_hl[:, HI, e, :], w1_raw[:, e, :], ACT.Copy).then_inc(s_w1hi, 1)
            for f in range(FT):
                router_h(0, f)
            score(0)
            for e in range(EXPERTS):
                act.activation(w2_hl[:, HI, e, :], w2_raw[:, e, :], ACT.Copy).then_inc(s_w2hi, 1)
            gate_exp(0)
            gate_hi(0, 0)
            gate_copy(0, 0)

            def phase(C, p, prep=True, first=False):
                q = 1 - p
                for k in range(SLOTS):
                    act.wait_ge(s_tt, C * SLOTS + k + 1)
                    if not (first and k < 4):
                        act.wait_ge(s_w2, C * SLOTS + k - 3)
                    act.activation(h_hl[:, k % 4, HI, :], tt[:, k % 4, :], ACT.Relu).then_inc(s_hhi, 1)
                    if k % FT == 1 and k + FT < SLOTS:
                        gate_copy(C, k // FT + 1)
                    if k == 2 and not first:
                        act.wait_ge(s_y, C)
                        act.activation(y_sb[:, :], yb[:, :], ACT.Copy).then_inc(s_ysb, 1)
                    if prep:
                        if k == AT_XT + 1:
                            x_hi(C + 1, q)
                        for f in range(FT):
                            if k == AT_R[f] + 1:
                                router_h(C + 1, f)
                        if k == AT_S + 2:
                            score(C + 1)
                        if k == AT_ST + 3:
                            gate_exp(C + 1)
                        if k == AT_GT + 1:
                            gate_hi(C + 1, q)
                        if k == SLOTS - 1:
                            gate_copy(C + 1, 0)

            phase(0, 0, first=True)
            with act.Fori(0, (CHUNKS - 2) // 2) as i:
                phase(i * 2 + 1, 1)
                phase(i * 2 + 2, 0)
            phase(CHUNKS - 1, 1, prep=False)
            act.wait_ge(s_y, CHUNKS)
            act.activation(y_sb[:, :], yb[:, :], ACT.Copy).then_inc(s_ysb, 1)

        @block.vector
        def _(dve):
            def low(out, x, hi, done):
                dve.tensor_tensor(out, x, hi.bitcast(f32), ALU.subtract).then_inc(done, 1)

            def tile(C, u):
                return x_sb[:, ds(C * TPC + u, 1), :].rearrange("p a d -> p (a d)")

            def moments(C):
                for u in range(TPC):
                    last = dve.bn_stats(bn[:, u, :], tile(C, u))
                last.then_inc(s_bn, 1)
                dve.wait_ge(s_bn, C + 1)
                dve.sem_inc(s_pass, 1)
                for u in range(TPC):
                    last = dve.bn_aggr(mv[:, u, :], bn[:, u, :])
                last.then_inc(s_mv, 1)
                dve.wait_ge(s_mv, C + 1)
                dve.tensor_scalar(mv[:, :, 1], mv[:, :, 1], EPS, None, ALU.add).then_inc(s_ve, 1)

            def normalise(C):
                dve.wait_ge(s_rstd, C + 1)
                for u in range(TPC):
                    last = dve.tensor_scalar(xn[:, u * D:(u + 1) * D], tile(C, u), mv[:, u, 0:1],
                                             rstd[:, u:u + 1], ALU.subtract, ALU.mult)
                last.then_inc(s_xn, 1)

            def x_lo(C, q):
                dve.wait_ge(s_xhi, C + 1)
                low(xT_hl[:, q, LO, :], mb[:, 0, :], xT_hl[:, q, HI, :], s_xlo)

            def over(a):
                return a.to_broadcast([P, TPC, EXPERTS])

            def top_two(C):
                dve.wait_ge(s_st, C + 1)
                dve.tensor_copy(s8[:, :, :], mb[:, 0, 0:TPC * EXPERTS]
                                .rearrange("p (u e) -> p u e", u=TPC)).then_inc(s_s8, 1)
                dve.wait_ge(s_s8, C + 1)
                dve.sem_inc(s_pass, 1)
                for u in range(TPC):
                    last = dve.max(top[:, u, :], s8[:, u, :])
                last.then_inc(s_top, 1)
                dve.wait_ge(s_top, C + 1)
                dve.tensor_tensor(shifted[:, :, :], s8[:, :, :], over(top[:, :, 0:1]),
                                  ALU.subtract).then_inc(s_sh, 1)
                for u in range(TPC):
                    last = dve.max_index(idx[:, u, :], top[:, u, :], s8[:, u, :])
                last.then_inc(s_idx, 1)
                dve.wait_ge(s_idx, C + 1)
                dve.tensor_copy(idxf[:, :, :], idx[:, :, :]).then_inc(s_idf, 1)
                dve.wait_ge(s_idf, C + 1)
                dve.tensor_tensor(is0[:, :, :], iota[:, :, :], over(idxf[:, :, 0:1]), ALU.is_equal)
                dve.tensor_tensor(is1[:, :, :], iota[:, :, :], over(idxf[:, :, 1:2]),
                                  ALU.is_equal).then_inc(s_eq, 1)
                dve.wait_ge(s_eq, C + 1)
                dve.tensor_tensor(mask[:, :, :], is0[:, :, :], is1[:, :, :], ALU.add).then_inc(s_mask, 1)

            def gates(C):
                dve.wait_ge(s_e8, C + 1)
                dve.wait_ge(s_mask, C + 1)
                dve.tensor_tensor(em[:, :, :], e8[:, :, :], mask[:, :, :], ALU.mult).then_inc(s_em, 1)
                dve.wait_ge(s_em, C + 1)
                dve.tensor_reduce(gsum[:, :], em[:, :, :], AX.X, ALU.add).then_inc(s_gs, 1)
                dve.wait_ge(s_gs, C + 1)
                dve.reciprocal(grcp[:, :], gsum[:, :]).then_inc(s_gr, 1)
                dve.wait_ge(s_gr, C + 1)
                r = grcp[:, :].rearrange("p (u a) -> p u a", a=1)
                dve.tensor_tensor(gpad[:, :, 0:EXPERTS], em[:, :, :], over(r), ALU.mult)
                dve.tensor_tensor(gpad[:, :, 32:32 + EXPERTS], em[:, :, :], over(r),
                                  ALU.mult).then_inc(s_g, 1)

            def gate_lo(C, q):
                dve.wait_ge(s_ghi, C + 1)
                rows = slice(32, 32 + EXPERTS)
                low(gT[rows, q, :], mb[rows, 1, :], gT[rows, q, :], s_glo)

            moments(0)
            dve.wait_ge(s_rwhi, 1)
            low(rw1_hl[:, LO, :], rw1_raw[:, :], rw1_hl[:, HI, :], s_rwlo)
            dve.wait_ge(s_b2hi, 1)
            low(b2_hl[:, LO, :], b2_raw[:, :], b2_hl[:, HI, :], s_b2lo)
            normalise(0)
            x_lo(0, 0)
            dve.wait_ge(s_pad, 1)
            dve.wait_ge(s_io, 1)
            top_two(0)
            gates(0)
            gate_lo(0, 0)

            def scale(C, k):
                if k % FT == 0:
                    dve.wait_ge(s_gbc, C * EXPERTS + k // FT + 1)
                dve.wait_ge(s_z, C * SLOTS + k + 1)
                dve.scalar_tensor_tensor(tt[:, k % 4, :], zb[:, k % 4, :], biasT[:, k:k + 1],
                                         gbc[:, k // FT % 2, :], ALU.add, ALU.mult).then_inc(s_tt, 1)

            def hidden_lo(C, k):
                dve.wait_ge(s_hhi, C * SLOTS + k + 1)
                dve.scalar_tensor_tensor(h_hl[:, k % 4, LO, :], tt[:, k % 4, :], 0.0,
                                         h_hl[:, k % 4, HI, :].bitcast(f32), ALU.max,
                                         ALU.subtract).then_inc(s_hlo, 1)

            def add_y(C):
                dve.wait_ge(s_yt, C + 1)
                tok = x_sb[:, ds(C * TPC, TPC), :].rearrange("p u d -> p (u d)")
                dve.tensor_tensor(tok, mb[:, 1, :], tok, ALU.add).then_inc(s_yadd, 1)

            def phase(C, p, prep=True, first=False):
                q = 1 - p
                for k in range(SLOTS):
                    scale(C, k)
                    if k > 0:
                        hidden_lo(C, k - 1)
                    elif not first:
                        hidden_lo(C - 1, SLOTS - 1)
                    if k == 4 and not first:
                        add_y(C - 1)
                    if prep:
                        if k == 0:
                            moments(C + 1)
                        if k == 3:
                            normalise(C + 1)
                        if k == AT_XT + 1:
                            x_lo(C + 1, q)
                        if k == AT_ST + 1:
                            top_two(C + 1)
                        if k == AT_ST + 4:
                            gates(C + 1)
                        if k == AT_GT + 2:
                            gate_lo(C + 1, q)

            phase(0, 0, first=True)
            with dve.Fori(0, (CHUNKS - 2) // 2) as i:
                phase(i * 2 + 1, 1)
                phase(i * 2 + 2, 0)
            phase(CHUNKS - 1, 1, prep=False)
            hidden_lo(CHUNKS - 1, SLOTS - 1)
            add_y(CHUNKS - 1)

        @block.tensor
        def _(pe):
            def product(out, lhs, rhs, start, stop):
                pe.matmul(out, lhs(HI), rhs(HI), start=start, stop=False)
                pe.matmul(out, lhs(HI), rhs(LO), start=False, stop=False)
                return pe.matmul(out, lhs(LO), rhs(HI), start=False, stop=stop)

            pe.transpose(gb[:, 0:NB], bias_raw[:, :], ident[0:NB, 0:NB]).then_inc(s_bt, 1)

            def x_transposes(C):
                pe.wait_ge(s_xn, C + 1)
                for u in range(TPC):
                    last = pe.transpose(mb[:, 0, u * P:(u + 1) * P], xn[:, u * D:(u + 1) * D], ident[:, :])
                last.then_inc(s_xt, 1)

            def router(C, q, f):
                if f == 0:
                    pe.wait_ge(s_xlo, C + 1)
                else:
                    if f >= 2:
                        pe.wait_ge(s_rh, C * FT + f - 1)
                product(mb[:, (f + 1) % 2, :], lambda a: rw1_hl[:, a, f * P:(f + 1) * P],
                        lambda a: xT_hl[:, q, a, :], True, True).then_inc(s_r, 1)

            def score(C):
                pe.wait_ge(s_rh, (C + 1) * FT)
                for f in range(FT):
                    last = pe.matmul(mb[0:EXPERTS, 1, :], rw2[:, f, :], rh[:, f, :],
                                     start=f == 0, stop=f == FT - 1)
                last.then_inc(s_s, 1)

            def score_transposes(C):
                pe.wait_ge(s_sT, C + 1)
                pe.sem_inc(s_pass, 1)
                for u in range(TPC):
                    last = pe.transpose(mb[:, 0, u * EXPERTS:(u + 1) * EXPERTS],
                                        sT[:, u * P:(u + 1) * P], ident[0:EXPERTS, 0:EXPERTS])
                last.then_inc(s_st, 1)

            def gate_transposes(C):
                pe.wait_ge(s_g, C + 1)
                for u in range(TPC):
                    last = pe.transpose(mb[:, 1, u * P:(u + 1) * P], gpad[:, u, :], ident[:, :])
                last.then_inc(s_gt, 1)

            def spread(C, p, e):
                if e == 0:
                    pe.wait_ge(s_glo, C + 1)
                else:
                    pe.wait_ge(s_gbc, C * EXPERTS + e)
                pe.matmul(gb[:, :], sel[:, e, :], gT[:, p, :], start=True, stop=True).then_inc(s_gb, 1)

            def first_product(C, p, k, first):
                if k % FT == 0 and first:
                    pe.wait_ge(s_w1lo, k // FT + 1)
                if not (first and k < 4):
                    pe.wait_ge(s_tt, C * SLOTS + k - 3)
                product(zb[:, k % 4, :], lambda a: w1_hl[:, a, k // FT, k % FT * P:(k % FT + 1) * P],
                        lambda a: xT_hl[:, p, a, :], True, True).then_inc(s_z, 1)

            def second_product(C, k, first):
                if k % FT == 0 and first:
                    pe.wait_ge(s_w2lo, k // FT + 1)
                if k == 0 and not first:
                    pe.wait_ge(s_ysb, C)
                pe.wait_ge(s_hlo, C * SLOTS + k + 1)
                product(yb[:, :], lambda a: w2_hl[:, a, k // FT, k % FT * D:(k % FT + 1) * D],
                        lambda a: h_hl[:, k % 4, a, :], k == 0, False).then_inc(s_w2, 1)

            def finish(C, p):
                pe.matmul(yb[:, :], b2_hl[:, HI, :], gT[:, p, :], start=False, stop=False)
                pe.matmul(yb[:, :], b2_hl[:, LO, :], gT[:, p, :], start=False, stop=True).then_inc(s_y, 1)

            def y_transposes(C):
                pe.wait_ge(s_ysb, C + 1)
                for u in range(TPC):
                    last = pe.transpose(mb[:, 1, u * P:(u + 1) * P], y_sb[:, u * P:(u + 1) * P], ident[:, :])
                last.then_inc(s_yt, 1)

            def phase(C, p, prep=True, first=False):
                q = 1 - p
                for k in range(SLOTS):
                    first_product(C, p, k, first)
                    if k % FT == 1 and k + FT < SLOTS:
                        spread(C, p, k // FT + 1)
                    if k >= LAG:
                        second_product(C, k - LAG, first)
                    elif not first:
                        second_product(C - 1, SLOTS - LAG + k, False)
                        if k == LAG - 1:
                            finish(C - 1, q)
                    if k == 4 and not first:
                        y_transposes(C - 1)
                    if prep:
                        if k == AT_XT:
                            x_transposes(C + 1)
                        for f in range(FT):
                            if k == AT_R[f]:
                                if f == 0 and not first:
                                    pe.wait_ge(s_yadd, C)
                                router(C + 1, q, f)
                        if k == AT_S:
                            score(C + 1)
                        if k == AT_ST:
                            score_transposes(C + 1)
                        if k == AT_GT:
                            gate_transposes(C + 1)
                        if k == SLOTS - 1:
                            spread(C + 1, q, 0)

            x_transposes(0)
            pe.wait_ge(s_rwlo, 1)
            for f in range(FT):
                router(0, 0, f)
            score(0)
            score_transposes(0)
            gate_transposes(0)
            pe.wait_ge(s_sel, 1)
            pe.wait_ge(s_bias, 1)
            pe.wait_ge(s_b2lo, 1)
            spread(0, 0, 0)
            phase(0, 0, first=True)
            with pe.Fori(0, (CHUNKS - 2) // 2) as i:
                phase(i * 2 + 1, 1)
                phase(i * 2 + 2, 0)
            phase(CHUNKS - 1, 1, prep=False)
            for k in range(SLOTS - LAG, SLOTS):
                second_product(CHUNKS - 1, k, False)
            finish(CHUNKS - 1, 1)
            y_transposes(CHUNKS - 1)


def build(nc, t):
    from concourse import mybir
    from contextlib import ExitStack

    f32 = mybir.dt.float32
    with ExitStack() as ctx:
        t["x_sb"] = ctx.enter_context(nc.sbuf_tensor("x_sb", [P, TILES, D], f32))
        t["ident"] = ctx.enter_context(nc.sbuf_tensor("ident", [P, P], f32))
        for name, shape in (("w1_raw", [P, EXPERTS, FF]), ("w2_raw", [P, EXPERTS, FF]),
                            ("rw1_raw", [P, FF]), ("rw2_sb", [P, FT, EXPERTS]),
                            ("bias_raw", [(EXPERTS + 1) * FT, P]), ("rb2_sb", [EXPERTS, 1]),
                            ("b2_raw", [GR, D])):
            t[name] = ctx.enter_context(nc.sbuf_tensor(name, shape, f32))
        attention(nc, t)
        experts(nc, t)


_INS = {"L0_attn_x": "x", "L0_attn_proj_q": "wq", "L0_attn_proj_k": "wk", "L0_attn_proj_v": "wv",
        "L0_attn_proj_o": "wo", "L0_ffn_rw1": "rw1", "L0_ffn_rb1": "rb1", "L0_ffn_rw2": "rw2",
        "L0_ffn_rb2": "rb2", "L0_ffn_W1": "W1", "L0_ffn_b1": "b1", "L0_ffn_W2": "W2", "L0_ffn_b2": "b2"}


def kernel(**inputs):
    import concourse.bacc as bacc
    from concourse import mybir
    from concourse.bass_utils import run_bass_kernel_spmd as run

    nc = bacc.Bacc("TRN2", target_bir_lowering=False, num_devices=1)
    arrays, t = {}, {}
    for name, short in _INS.items():
        a = np.ascontiguousarray(inputs[name])
        arrays[name] = a
        t[short] = nc.dram_tensor(name, a.shape, mybir.dt.from_np(a.dtype), kind="ExternalInput").ap()
    t["out"] = nc.dram_tensor("out", (B, N, D), mybir.dt.float32, kind="ExternalOutput").ap()
    build(nc, t)
    return run(nc, [arrays], core_ids=[0]).results[0]["out"]
```

```python
import numpy as np

B, N, D = 2, 2048, 128
HEADS = 8
P = 128
EPS = 1e-5
FF = 512
EXPERTS = 8
CH = 512
TPC = CH // P
TPB = N // P
CPB = N // CH
GPB = CPB * HEADS
TILES = B * TPB
CHUNKS = B * CPB
FT = FF // P
HI, LO = 0, 1
NB = (EXPERTS + 1) * FT
GR = 64


def attention(nc, t, rt):
    import concourse.bass as bass
    from concourse import mybir
    from contextlib import ExitStack

    f32, f32r = mybir.dt.float32, mybir.dt.float32r
    ALU, ACT, AX = mybir.AluOpType, mybir.ActivationFunctionType, mybir.AxisListType
    ds = bass.ds
    x_sb, ident = t["x_sb"], t["ident"]
    SP = 96
    YW = D + 2
    AHEAD = 3
    PV_LAG = 3
    AT_COPY, AT_O, AT_Y, AT_G, AT_MAX = 4, 3, 6, 10, 14
    PREP = 5
    AT_XT = ((4, 13), (3, 1), (3, 13), (2, 1))
    AT_VHI = ((4, 11), (4, 15), (3, 3), (3, 7))
    AT_VLO = ((3, 8), (2, 8), (1, 2), (1, 8))
    AT_WO, AT_M, AT_FIRST_VLO = 1, 6, (None, 5, 9, 11)
    AT_RT_BN, AT_RT_NORM, AT_RT_RW = (2, 0), (2, 10), (2, 8)
    AT_RT_XT, AT_RT_R, AT_RT_S, AT_RT_ST = (1, 0), ((1, 3), (1, 4), (1, 5), (1, 6)), (1, 8), (1, 10)
    AT_RT_G = (1, 11)
    AT_NORM = 5

    with ExitStack() as ctx:
        def sb(name, shape, dt=f32):
            return ctx.enter_context(nc.sbuf_tensor(name, shape, dt))

        def pb(name, shape):
            return ctx.enter_context(nc.psum_tensor(name, shape, f32))

        def sem(name):
            return ctx.enter_context(nc.semaphore(name))

        rh_heads = rt.rh[:, :, :].rearrange("p c (h d) -> p (c h) d", d=D)
        wo_raw = rh_heads[:, 0:HEADS, :]
        lhs_f = rh_heads[:, HEADS:, :]
        wkv_raw, kv_f = rt.gpad[:, 0:2, :], rt.gpad[:, 2:4, :]
        kv_hl = sb("kv_hl", [P, 2, 2, D], f32r)
        a_hl = sb("a_hl", [P, HEADS, 2, D], f32r)
        a_cur = sb("a_cur", [P, 2, 2, D], f32r)
        m_hl = sb("m_hl", [P, 2, HEADS, YW], f32r)
        bn = sb("bn", [P, TPB, 6])
        mv = sb("mv", [P, TPB, 2])
        mhalf = sb("mhalf", [P, TPB])
        rstd = sb("rstd", [P, TPB])
        xn = sb("xn", [P, TPB, D])
        val_hl = sb("val_hl", [P, B, 2, TPB, D], f32r)
        key_hl = sb("key_hl", [P, B, 2, N], f32r)
        spare = val_hl[:, B - 1, :, :, :].rearrange("p a (i h) d -> p (a i) h d", h=HEADS)
        lhs_hl, woT_hl = spare[:, 0:2, :, :], spare[:, 2:4, :, :]
        rt.xn = xn[:, 0:TPC, :].rearrange("p n d -> p (n d)")
        rt.sT = xn[0:EXPERTS, TPC:2 * TPC, :].rearrange("p n d -> p (n d)")
        new_hi = sb("new_hi", [P, 2, CH], f32r)
        new_lo = sb("new_lo", [P, CH], f32r)
        q_hl = sb("q_hl", [P, 2, 2, CH], f32r)
        mx = sb("mx", [P, 2, TPC, CPB])
        pad = sb("pad", [P, TPC, P])
        pf = sb("pf", [P, 4, CH])
        wq_raw = pf[:, 0:2, :].rearrange("p c (h d) -> p (c h) d", d=D)
        pt_hl = sb("pt_hl", [P, 4, 2, CH], f32r)
        oT_hl = sb("oT_hl", [P, 2, CH], f32r)
        rcp = sb("rcp", [P, TPC])

        st = pb("st", [P, 2, CH])
        mp = pb("mp", [P, 2, CH])
        rt.mb = mp
        ob = pb("ob", [P, 2, CH])
        wb = pb("wb", [P, 2, CH])

        s_x, s_w = sem("x_loaded"), sem("w_loaded")
        s_b2c, s_ffn = sem("b2_cleared"), sem("ffn_loaded")
        s_id0, s_id = sem("ident_cleared"), sem("ident_ready")
        s_mh, s_pad, s_pick = sem("mhalf_ready"), sem("pad_cleared"), sem("m_pick_ready")
        s_pass = sem("passed")
        s_wt, s_wf = sem("weights_transposed"), sem("weights_reduced")
        s_whi, s_wlo = sem("weights_hi"), sem("weights_lo")
        s_a, s_ahi, s_alo = sem("a_folded"), sem("a_hi"), sem("a_lo")
        s_wo, s_wot, s_wohi, s_wolo = sem("wo_loaded"), sem("wo_transposed"), sem("wo_hi"), sem("wo_lo")
        s_m, s_mhi, s_mlo = sem("m_folded"), sem("m_hi"), sem("m_lo")
        s_bn, s_mv, s_ve = sem("bn_stats"), sem("mean_var"), sem("var_eps")
        s_rstd, s_xn, s_one = sem("rstd_ready"), sem("xn_ready"), sem("xn_one")
        s_vhi, s_vlo = sem("val_hi"), sem("val_lo")
        s_xt, s_xhi, s_xlo = sem("xn_transposed"), sem("xT_hi"), sem("xT_lo")
        s_ac = sem("a_copied")
        s_q, s_nhi, s_nlo = sem("queries_done"), sem("new_hi_ready"), sem("new_lo_ready")
        s_clo = sem("q_lo_copied")
        s_mp, s_mx, s_nm = sem("max_scores"), sem("tile_max"), sem("row_max")
        s_mt, s_row = sem("max_transposed"), sem("shift_in_q")
        s_st, s_hi, s_lo = sem("scores_done"), sem("exp_hi"), sem("exp_lo")
        s_pv, s_ohi, s_olo = sem("pv_done"), sem("o_hi"), sem("o_lo")
        s_y, s_rcp, s_yadd = sem("y_done"), sem("rcp_ready"), sem("y_added")

        def xt_bank(b, c):
            if b == 0:
                return (wb if c < 2 else ob)[:, c % 2, :]
            return wb[:, 0, :]

        def mp_bank(first, n):
            return (mp if not first or n % 4 < 2 else ob)[:, n % 2, :]

        def by_head(banks):
            return banks[:, :, :].rearrange("p c (h d) -> p (c h) d", d=D)

        s_se0, s_se1, s_iu = sem("sel_cleared"), sem("sel_half"), sem("iota_made")

        block = ctx.enter_context(nc.Block())

        @block.sync
        def _(sp):
            for b in range(B):
                if b > 0:
                    sp.wait_ge(s_x, 16 * b)
                sp.dma_start(x_sb[:, b * TPB:(b + 1) * TPB, :],
                             t["x"][b, :, :].rearrange("(n p) d -> p n d", p=P)).then_inc(s_x, 16)
            sp.dma_start(rt.rw1_raw[:, :], t["rw1"]).then_inc(s_ffn, 16)
            sp.dma_start(rt.rw2[:, :, :], t["rw2"].rearrange("(f p) e -> p f e", p=P)).then_inc(s_ffn, 16)
            sp.dma_start(rt.bias_raw[0:EXPERTS * FT, :],
                         t["b1"].rearrange("e (f p) -> (e f) p", p=P)).then_inc(s_ffn, 16)
            sp.dma_start(rt.bias_raw[EXPERTS * FT:(EXPERTS + 1) * FT, :],
                         t["rb1"].rearrange("(f p) -> f p", p=P)).then_inc(s_ffn, 16)
            sp.dma_start(rt.rb2[:, :], t["rb2"].partition_broadcast(P)).then_inc(s_ffn, 16)
            sp.wait_ge(s_b2c, 1)
            for row in (0, GR // 2):
                sp.dma_start(t["b2_raw"][row:row + EXPERTS, :], t["b2"]).then_inc(s_ffn, 16)
            sp.dma_start(t["w1_raw"][:, :, :], t["W1"].rearrange("e d f -> d e f")).then_inc(s_ffn, 16)
            sp.wait_ge(s_ffn, 8 * 16)

        @block.gpsimd
        def _(pool):
            pool.memset(ident[:, :], 0.0).then_inc(s_id0, 1)
            pool.memset(mhalf[:, :], -0.5).then_inc(s_mh, 1)
            pool.memset(t["b2_raw"][:, :], 0.0).then_inc(s_b2c, 1)
            pool.wait_ge(s_id0, 1)
            pool.affine_select(out=ident[:, :], in_=ident[:, :], compare_op=ALU.not_equal, fill=1.0,
                               base=0, pattern=[[-1, P]], channel_multiplier=1).then_inc(s_id, 1)
            pool.memset(pad[:, :, :], 0.0).then_inc(s_pad, 1)
            pool.memset(m_hl[:, :, :, D:YW].bitcast(f32), 0.0).then_inc(s_pick, 1)
            pool.wait_ge(s_mh, 1)

            def copy_a(head, parity):
                pool.tensor_copy(a_cur[:, parity, :, :].rearrange("p a n -> p (a n)"),
                                 a_hl[:, ds(head, 1), :, :].bitcast(f32)
                                 .rearrange("p h a n -> p (h a n)")).then_inc(s_ac, 1)

            def phase(G, head, parity):
                pool.wait_ge(s_q, G + 1)
                pool.sem_inc(s_pass, 1)
                copy_a(head, parity)

            def routing_constants():
                pool.wait_ge(s_mlo, 1)
                pool.memset(rt.gpad[:, :, :], 0.0).then_inc(rt.s_pad, 1)
                sel_f = rt.rh[0:GR, 0:2, :].rearrange("p c (e n) -> p (c e) n", n=P)
                pool.memset(sel_f, 0.0).then_inc(s_se0, 1)
                for half, (before, after) in enumerate(((s_se0, s_se1), (s_se1, s_se1))):
                    pool.wait_ge(before, 1)
                    pool.affine_select(out=sel_f, in_=sel_f, compare_op=ALU.not_equal,
                                       fill=1.0, base=-32 * half, pattern=[[-1, EXPERTS], [0, P]],
                                       channel_multiplier=1).then_inc(after, 1)
                pool.wait_ge(s_se1, 2)
                pool.tensor_copy(rt.sel[:, :, :], sel_f)
                pool.iota(rt.iota_u[:, :, :], pattern=[[0, TPC], [1, EXPERTS]], base=0,
                          channel_multiplier=0).then_inc(s_iu, 1)
                pool.wait_ge(s_iu, 1)
                pool.tensor_copy(rt.iota[:, :, :], rt.iota_u[:, :, :]).then_inc(rt.s_io, 1)

            def power(b):
                pool.wait_ge(s_ve, b + 1)
                pool.tensor_tensor(rstd[:, :], mv[:, :, 1], mhalf[:, :], ALU.pow).then_inc(s_rstd, 1)

            power(0)
            pool.wait_ge(s_ahi, 2)
            pool.wait_ge(s_alo, 1)
            for b in range(B):
                for part, (start, stop) in enumerate(((0, GPB - PREP + 1), (GPB - PREP + 1, GPB))):
                    if part == 1 and b + 1 < B:
                        power(b + 1)
                    if part == 1 and b == 0:
                        routing_constants()
                    if b + 1 == B:
                        stop = min(stop, GPB - 2)
                    with pool.Fori(0, (stop - start) // 2) as i:
                        phase(b * GPB + start + i * 2, (i * 2 + start + 2) & (HEADS - 1), 0)
                        phase(b * GPB + start + i * 2 + 1, (i * 2 + start + 3) & (HEADS - 1), 1)
            routing_gpsimd(pool, rt, mhalf)(0)

        @block.scalar
        def _(act):
            act.dma_start(wkv_raw[:, 0, :], t["wk"]).then_inc(s_w, 16)
            act.dma_start(wkv_raw[:, 1, :], t["wv"]).then_inc(s_w, 16)
            act.dma_start(wq_raw[:, :, :], t["wq"].rearrange("h d k -> d h k")).then_inc(s_w, 16)
            act.dma_start(wo_raw[:, :, :], t["wo"].rearrange("h d v -> d h v")).then_inc(s_wo, 16)
            act.wait_ge(s_wf, 1)
            act.activation(lhs_hl[:, HI, :, :], lhs_f[:, :, :], ACT.Copy)
            act.activation(kv_hl[:, HI, :, :], kv_f[:, :, :], ACT.Copy).then_inc(s_whi, 1)

            def first_a_hi():
                act.wait_ge(s_a, 1)
                act.activation(a_cur[:, :, HI, :], by_head(st)[:, 0:2, :], ACT.Copy).then_inc(s_ahi, 1)

            def all_a_hi():
                act.wait_ge(s_a, 2)
                act.activation(a_hl[:, :, HI, :], by_head(st), ACT.Copy).then_inc(s_ahi, 1)

            def val_hi(b, c):
                act.wait_ge(s_one, b * CPB + c + 1)
                act.activation(val_hl[:, b, HI, c * TPC:(c + 1) * TPC, :],
                               xn[:, c * TPC:(c + 1) * TPC, :], ACT.Copy).then_inc(s_vhi, 1)

            def xt_hi(b, c):
                act.wait_ge(s_xt, b * CPB + c + 1)
                act.activation(key_hl[:, b, HI, c * CH:(c + 1) * CH], xt_bank(b, c),
                               ACT.Copy).then_inc(s_xhi, 1)

            def new_queries_hi(G, k):
                act.wait_ge(s_q, G + 1)
                act.activation(new_hi[:, k % 2, :], wb[:, 0, :], ACT.Copy).then_inc(s_nhi, 1)

            def copy_q_hi(G, k):
                act.wait_ge(s_nhi, G + 1)
                act.activation(q_hl[:, k % 2, HI, :], new_hi[:, k % 2, :].bitcast(f32),
                               ACT.Copy)

            def shift_row(G, k):
                act.wait_ge(s_mt, G + 1)
                act.activation(q_hl[SP:SP + 1, k % 2, HI, :], wb[SP:SP + 1, 1, :],
                               ACT.Copy).then_inc(s_row, 1)

            def exps(G, tile, fresh=False):
                act.wait_ge(s_st, G * TPB + tile + 1)
                if not fresh:
                    act.wait_ge(s_pv, G * TPB + tile - 3)
                act.activation(pf[:, tile % 4, :], st[:, tile % 2, :], ACT.Exp)
                act.activation(pt_hl[:, tile % 4, HI, :], st[:, tile % 2, :], ACT.Exp).then_inc(s_hi, 1)

            def o_hi(G, p):
                act.wait_ge(s_pv, (G + 1) * TPB)
                act.activation(oT_hl[:, HI, :], ob[:, p, :], ACT.Copy).then_inc(s_ohi, 1)

            steps = routing_scalar(act, rt)

            def route(togo, s):
                at, before = (togo, s), (togo, s - 1)
                if at == AT_RT_RW:
                    act.wait_ge(s_ffn, 8 * 16)
                    act.activation(rt.rw1_hl[:, HI, :], rt.rw1_raw[:, :], ACT.Copy).then_inc(rt.s_rwhi, 1)
                if before == AT_RT_XT:
                    act.wait_ge(rt.s_bt, 1)
                    act.activation(rt.biasT[:, :], mp[:, 1, 0:NB], ACT.Copy).then_inc(rt.s_bias, 1)
                    steps.x_hi(0, 0)
                    act.wait_ge(rt.s_bias, 1)
                for f in range(FT):
                    if at == AT_RT_R[f]:
                        steps.router_h(0, f)
                if at == AT_RT_S:
                    steps.score(0)
                if before == AT_RT_G:
                    steps.gate_exp(0)

            def phase(G, p, first=False, following=True, queries=True, prep=0, togo=0):
                q = 1 - p
                for s in range(TPB):
                    exps(G, s, fresh=first and s < 4)
                    if s == AT_O and not first:
                        o_hi(G - 1, q)
                    if s == AT_COPY and following:
                        copy_q_hi(G + 1, q)
                    if s == AT_G and queries:
                        new_queries_hi(G + 2, p)
                    if s == AT_MAX and following:
                        shift_row(G + 1, q)
                    if first and s == AT_WO + 1:
                        act.wait_ge(s_wot, 1)
                        act.activation(woT_hl[:, HI, :, :], by_head(wb), ACT.Copy).then_inc(s_wohi, 1)
                    if first and s == AT_M + 1:
                        act.wait_ge(s_m, 1)
                        act.activation(m_hl[:, HI, :, 0:D], by_head(wb), ACT.Copy).then_inc(s_mhi, 1)
                    if togo and not prep:
                        route(togo, s)
                    for c in range(CPB):
                        if prep and (togo, s) == AT_VHI[c]:
                            val_hi(prep, c)
                        if prep and (togo, s - 1) == AT_XT[c]:
                            xt_hi(prep, c)

            xt_hi(0, 0)
            xt_hi(0, 1)
            first_a_hi()
            xt_hi(0, 2)
            xt_hi(0, 3)
            new_queries_hi(0, 0)
            copy_q_hi(0, 0)
            new_queries_hi(1, 1)
            all_a_hi()
            for c in range(CPB):
                val_hi(0, c)
            shift_row(0, 0)
            for b in range(B):
                phase(b * GPB, 0, first=b == 0)
                with act.Fori(0, (GPB - 1 - PREP) // 2) as i:
                    phase(b * GPB + i * 2 + 1, 1)
                    phase(b * GPB + i * 2 + 2, 0)
                for togo in range(PREP, 0, -1):
                    phase((b + 1) * GPB - togo, togo % 2, following=togo > 1 or b + 1 < B,
                          queries=togo > 2 or b + 1 < B, prep=(b + 1) % B, togo=togo)
            steps.gate_hi(0, 0)
            o_hi(B * GPB - 1, 1)

        @block.vector
        def _(dve):
            def low(out, x, hi):
                return dve.tensor_tensor(out, x, hi.bitcast(f32), ALU.subtract)

            dve.wait_ge(s_pick, 1)
            dve.memset(m_hl[SP:SP + 1, HI, :, D:D + 1].bitcast(f32), 1.0).then_inc(s_pick, 1)

            def reduce_weights():
                dve.wait_ge(s_wt, 1)
                for h in range(HEADS):
                    src = by_head(st)[:, h, :]
                    dve.tensor_scalar(lhs_f[:, h, :], src, src[:, SP:SP + 1], None, ALU.subtract)
                for n in range(2):
                    src = wb[:, 0, n * D:(n + 1) * D]
                    last = dve.tensor_scalar(kv_f[:, n, :], src, src[:, SP:SP + 1], None, ALU.subtract)
                last.then_inc(s_wf, 1)

            def weights_lo():
                dve.wait_ge(s_whi, 1)
                low(lhs_hl[:, LO, :, :], lhs_f[:, :, :], lhs_hl[:, HI, :, :])
                low(kv_hl[:, LO, :, :], kv_f[:, :, :], kv_hl[:, HI, :, :]).then_inc(s_wlo, 1)

            def first_a_lo():
                dve.wait_ge(s_ahi, 1)
                low(a_cur[:, :, LO, :], by_head(st)[:, 0:2, :], a_cur[:, :, HI, :]).then_inc(s_ac, 2)

            def all_a_lo():
                dve.wait_ge(s_ahi, 2)
                low(a_hl[:, :, LO, :], by_head(st), a_hl[:, :, HI, :]).then_inc(s_alo, 1)

            def new_queries_lo(G, k):
                dve.wait_ge(s_nhi, G + 1)
                low(new_lo[:, :], wb[:, 0, :], new_hi[:, k % 2, :]).then_inc(s_nlo, 1)

            def copy_q_lo(G, k):
                dve.wait_ge(s_nlo, G + 1)
                dve.tensor_copy(q_hl[:, k % 2, LO, :], new_lo[:, :].bitcast(f32)).then_inc(s_clo, 1)

            def tile_max(G, k, n, first=False):
                dve.wait_ge(s_mp, G * TPB + n + 1)
                dve.tensor_reduce(mx[:, k, n // CPB, n % CPB:n % CPB + 1], mp_bank(first, n), AX.X,
                                  ALU.max).then_inc(s_mx, 1)

            def row_max(G, k):
                dve.wait_ge(s_mx, (G + 1) * TPB)
                dve.tensor_reduce(pad[:, :, SP], mx[:, k, :, :], AX.X, ALU.max,
                                  negate=True).then_inc(s_nm, 1)

            def exp_lo(G, tile):
                dve.wait_ge(s_hi, G * TPB + tile + 1)
                low(pt_hl[:, tile % 4, LO, :], pf[:, tile % 4, :], pt_hl[:, tile % 4, HI, :])\
                    .then_inc(s_lo, 1)

            def o_lo(G, p):
                dve.wait_ge(s_ohi, G + 1)
                low(oT_hl[:, LO, :], ob[:, p, :], oT_hl[:, HI, :]).then_inc(s_olo, 1)

            def y_add(G, tile0):
                dve.wait_ge(s_y, G + 1)
                units = wb[:, :, 0:2 * YW].rearrange("p c (u w) -> p c u w", w=YW)
                dve.reciprocal(rcp[:, :].rearrange("p (c u) -> p c u", u=2),
                               units[:, :, :, D]).then_inc(s_rcp, 1)
                dve.wait_ge(s_rcp, G + 1)
                for u in range(TPC):
                    tok = x_sb[:, ds(tile0 + u, 1), :].rearrange("p a d -> p (a d)")
                    last = dve.scalar_tensor_tensor(tok, units[:, u // 2, u % 2, 0:D],
                                                    rcp[:, u:u + 1], tok, ALU.mult, ALU.add)
                last.then_inc(s_yadd, 1)

            def stats(b, n):
                last = dve.bn_stats(bn[:, n, :], x_sb[:, b * TPB + n, :])
                if n == TPB - 1:
                    last.then_inc(s_bn, 1)

            def mean_var(b, half):
                dve.wait_ge(s_bn, b + 1)
                for n in range(half * TPB // 2, (half + 1) * TPB // 2):
                    last = dve.bn_aggr(mv[:, n, :], bn[:, n, :])
                if half == 1:
                    last.then_inc(s_mv, 1)

            def add_eps(b):
                dve.wait_ge(s_mv, b + 1)
                dve.tensor_scalar(mv[:, :, 1], mv[:, :, 1], EPS, None, ALU.add).then_inc(s_ve, 1)

            def normalise(b, n):
                dve.wait_ge(s_rstd, b + 1)
                last = dve.tensor_scalar(xn[:, n, :], x_sb[:, b * TPB + n, :],
                                         mv[:, n, 0:1], rstd[:, n:n + 1], ALU.subtract, ALU.mult)
                if n % TPC == TPC - 1:
                    last.then_inc(s_xn, 1)

            def set_one(b, c):
                dve.wait_ge(s_xn, b * CPB + c + 1)
                dve.memset(xn[:, c * TPC:(c + 1) * TPC, SP:SP + 1], 1.0).then_inc(s_one, 1)

            def val_lo(b, c):
                dve.wait_ge(s_vhi, b * CPB + c + 1)
                low(val_hl[:, b, LO, c * TPC:(c + 1) * TPC, :], xn[:, c * TPC:(c + 1) * TPC, :],
                    val_hl[:, b, HI, c * TPC:(c + 1) * TPC, :]).then_inc(s_vlo, 1)

            def key_lo(b, c):
                dve.wait_ge(s_xhi, b * CPB + c + 1)
                low(key_hl[:, b, LO, c * CH:(c + 1) * CH], xt_bank(b, c),
                    key_hl[:, b, HI, c * CH:(c + 1) * CH]).then_inc(s_xlo, 1)

            def prepare(b, togo, s):
                if togo == 5:
                    stats(b, s)
                if togo == 4 and s < 2:
                    mean_var(b, s)
                if togo == 4 and s == 2:
                    add_eps(b)
                n = (4 - togo) * TPB + s - AT_NORM
                if 0 <= n < TPB:
                    normalise(b, n)
                if n > 0 and n % TPC == 0 and n <= TPB:
                    set_one(b, n // TPC - 1)
                for c in range(CPB):
                    if (togo, s) == AT_VLO[c]:
                        val_lo(b, c)
                    if (togo, s - 2) == AT_XT[c]:
                        key_lo(b, c)

            steps = routing_vector(dve, rt, x_sb)

            def route(togo, s):
                at, before = (togo, s), (togo, s - 1)
                if togo == AT_RT_BN[0] and 0 <= s - AT_RT_BN[1] < 3:
                    steps.moments(0, s - AT_RT_BN[1])
                if togo == AT_RT_NORM[0] and 0 <= s - AT_RT_NORM[1] < TPC:
                    steps.normalise(0, s - AT_RT_NORM[1])
                if before == AT_RT_RW:
                    dve.wait_ge(rt.s_rwhi, 1)
                    low(rt.rw1_hl[:, LO, :], rt.rw1_raw[:, :], rt.rw1_hl[:, HI, :]).then_inc(rt.s_rwlo, 1)
                if before == AT_RT_XT:
                    steps.x_lo(0, 0)
                if at == AT_RT_G:
                    dve.wait_ge(rt.s_pad, 1)
                    dve.wait_ge(rt.s_io, 1)
                if togo == AT_RT_G[0] and 0 <= s - AT_RT_G[1] < 5:
                    steps.gates(0, 2 * (s - AT_RT_G[1]))
                    steps.gates(0, 2 * (s - AT_RT_G[1]) + 1)

            def phase(G, p, tile0, first=False, following=True, queries=True, prep=0, togo=0):
                q = 1 - p
                for s in range(TPB):
                    n = s + AHEAD
                    if n < TPB and following:
                        tile_max(G + 1, q, n)
                    elif n >= TPB and queries:
                        tile_max(G + 2, p, n - TPB)
                    if s > 0:
                        exp_lo(G, s - 1)
                    elif not first:
                        exp_lo(G - 1, TPB - 1)
                    if n == TPB - 1 and following:
                        row_max(G + 1, q)
                    if s == AT_O and not first:
                        o_lo(G - 1, q)
                    if s == AT_COPY and following:
                        copy_q_lo(G + 1, q)
                    if s == AT_Y and not first:
                        y_add(G - 1, tile0)
                    if s == AT_G and queries:
                        new_queries_lo(G + 2, p)
                    if first and s == AT_WO + 2:
                        dve.wait_ge(s_wohi, 1)
                        low(woT_hl[:, LO, :, :], by_head(wb), woT_hl[:, HI, :, :]).then_inc(s_wolo, 1)
                    if first and s == AT_M + 2:
                        dve.wait_ge(s_mhi, 1)
                        low(m_hl[:, LO, :, 0:D], by_head(wb), m_hl[:, HI, :, 0:D]).then_inc(s_mlo, 1)
                    if first and s in AT_FIRST_VLO:
                        val_lo(0, AT_FIRST_VLO.index(s))
                    if prep:
                        prepare(prep, togo, s)
                    elif togo:
                        route(togo, s)

            dve.wait_ge(s_x, 16)
            for n in range(TPB):
                stats(0, n)
            mean_var(0, 0)
            mean_var(0, 1)
            add_eps(0)
            reduce_weights()
            for c in range(CPB):
                for n in range(c * TPC, (c + 1) * TPC):
                    normalise(0, n)
                set_one(0, c)
                if c == 1:
                    weights_lo()
            key_lo(0, 0)
            first_a_lo()
            for c in range(1, CPB):
                key_lo(0, c)
            new_queries_lo(0, 0)
            copy_q_lo(0, 0)
            dve.wait_ge(s_pad, 1)
            for n in range(TPB):
                if n == 4:
                    dve.wait_ge(s_clo, 1)
                    new_queries_lo(1, 1)
                if n == 10:
                    all_a_lo()
                tile_max(0, 0, n, first=True)
            row_max(0, 0)
            for n in range(AHEAD):
                tile_max(1, 1, n)
            val_lo(0, 0)
            dve.wait_ge(s_x, 16 * B)
            for b in range(B):
                T0 = b * TPB
                last_chunk = TPB - TPC
                phase(b * GPB, 0, T0 - TPC, first=b == 0)
                with dve.Fori(0, (GPB - 1 - PREP) // 2) as i:
                    phase(b * GPB + i * 2 + 1, 1, T0 + (i & last_chunk))
                    phase(b * GPB + i * 2 + 2, 0, T0 + (i & last_chunk))
                for togo in range(PREP, 0, -1):
                    phase((b + 1) * GPB - togo, togo % 2, T0 + last_chunk,
                          following=togo > 1 or b + 1 < B, queries=togo > 2 or b + 1 < B,
                          prep=(b + 1) % B, togo=togo)
            exp_lo(B * GPB - 1, TPB - 1)
            steps.gate_lo(0, 0)
            o_lo(B * GPB - 1, 1)
            y_add(B * GPB - 1, B * TPB - TPC)

        @block.tensor
        def _(pe):
            def product(out, lhs, rhs, start, stop):
                pe.matmul(out, lhs(HI), rhs(HI), start=start, stop=False)
                pe.matmul(out, lhs(HI), rhs(LO), start=False, stop=False)
                return pe.matmul(out, lhs(LO), rhs(HI), start=False, stop=stop)

            def weight_transposes():
                pe.wait_ge(s_id, 1)
                pe.wait_ge(s_w, 3 * 16)
                for h in range(HEADS):
                    pe.transpose(by_head(st)[:, h, :], wq_raw[:, h, :], ident[:, :])
                for n in range(2):
                    last = pe.transpose(wb[:, 0, n * D:(n + 1) * D], wkv_raw[:, n, :], ident[:, :])
                last.then_inc(s_wt, 1)

            def fold_a(heads):
                for h in heads:
                    last = product(by_head(st)[:, h, :], lambda a: lhs_hl[:, a, h, :],
                                   lambda a: kv_hl[:, a, 0, :], True, True)
                last.then_inc(s_a, 1)

            def wo_transposes():
                pe.wait_ge(s_wo, 16)
                pe.wait_ge(s_nlo, 2)
                for h in range(HEADS):
                    last = pe.transpose(by_head(wb)[:, h, :], wo_raw[:, h, :], ident[:, :])
                last.then_inc(s_wot, 1)

            def fold_m():
                pe.wait_ge(s_wolo, 1)
                for c in range(2):
                    last = product(wb[:, c, :], lambda a: kv_hl[:, a, 1, :],
                                   lambda a: woT_hl[:, a, c * TPC:(c + 1) * TPC, :], True, True)
                last.then_inc(s_m, 1)

            def x_transposes(b, c):
                pe.wait_ge(s_one, b * CPB + c + 1)
                for u in range(TPC):
                    last = pe.transpose(xt_bank(b, c)[:, u * P:(u + 1) * P], xn[:, c * TPC + u, :],
                                        ident[:, :])
                last.then_inc(s_xt, 1)

            def queries(b, G, k, col):
                pe.wait_ge(s_ac, G + 1)
                product(wb[:, 0, :], lambda a: a_cur[:, k % 2, a, :],
                        lambda a: key_hl[:, b, a, ds(col, CH)], True, True).then_inc(s_q, 1)

            def max_scores(b, G, k, n, first=False):
                if n == 0:
                    pe.wait_ge(s_nhi, G + 1)
                if not first:
                    pe.wait_ge(s_mx, G * TPB + n - 1)
                elif n >= 4:
                    pe.wait_ge(s_mx, n - 3)
                unit, c = n // CPB, n % CPB
                pe.matmul(mp_bank(first, n), new_hi[:, k % 2, unit * P:(unit + 1) * P],
                          key_hl[:, b, HI, c * CH:(c + 1) * CH], start=True, stop=True).then_inc(s_mp, 1)

            def max_transposes(G):
                pe.wait_ge(s_nm, G + 1)
                for u in range(TPC):
                    last = pe.transpose(wb[:, 1, u * P:(u + 1) * P], pad[:, u, :], ident[:, :])
                last.then_inc(s_mt, 1)

            def scores(b, G, p, tile, fresh=False):
                if tile == 0:
                    pe.wait_ge(s_clo, G + 1)
                    pe.wait_ge(s_row, G + 1)
                if not fresh:
                    pe.wait_ge(s_hi, G * TPB + tile - 1)
                product(st[:, tile % 2, :], lambda a: key_hl[:, b, a, tile * P:(tile + 1) * P],
                        lambda a: q_hl[:, p, a, :], True, True).then_inc(s_st, 1)

            def pv(b, G, p, tile):
                pe.wait_ge(s_lo, G * TPB + tile + 1)
                product(ob[:, p, :], lambda a: val_hl[:, b, a, tile, :],
                        lambda a: pt_hl[:, tile % 4, a, :],
                        tile == 0, tile == TPB - 1).then_inc(s_pv, 1)

            def project(G, head):
                pe.wait_ge(s_olo, G + 1)
                for u in range(TPC):
                    last = product(wb[:, u // 2, u % 2 * YW:(u % 2 + 1) * YW],
                                   lambda a: oT_hl[:, a, u * P:(u + 1) * P],
                                   lambda a: m_hl[:, a, ds(head, 1), :].rearrange("p h w -> p (h w)"),
                                   True, True)
                last.then_inc(s_y, 1)

            steps = routing_tensor(pe, rt, ident)

            def route(togo, s):
                at = (togo, s)
                if at == AT_RT_XT:
                    pe.wait_ge(s_mx, B * GPB * TPB)
                    pe.wait_ge(s_ffn, 8 * 16)
                    pe.transpose(mp[:, 1, 0:NB], rt.bias_raw[:, :], ident[0:NB, 0:NB]).then_inc(rt.s_bt, 1)
                    steps.x_transposes(0)
                for f in range(FT):
                    if at == AT_RT_R[f]:
                        if f == 0:
                            pe.wait_ge(rt.s_rwlo, 1)
                            pe.wait_ge(rt.s_bias, 1)
                        steps.router(0, 0, f)
                if at == AT_RT_S:
                    steps.score(0)
                if at == AT_RT_ST:
                    steps.score_transposes(0)

            def phase(batches, G, p, head, col, first=False, following=True, queries_=True,
                      prep=0, togo=0):
                q = 1 - p
                before, b, after, after2 = batches
                for s in range(TPB):
                    scores(b, G, p, s, fresh=first and s < 2)
                    n = s + AHEAD
                    if n < TPB and following:
                        max_scores(after, G + 1, q, n)
                    elif n >= TPB and queries_:
                        max_scores(after2, G + 2, p, n - TPB)
                    if s >= PV_LAG:
                        if b != before and s == PV_LAG:
                            pe.wait_ge(s_vlo, (b + 1) * CPB)
                        if first and (s - PV_LAG) % TPC == 0:
                            pe.wait_ge(s_vlo, (s - PV_LAG) // TPC + 1)
                        pv(b, G, p, s - PV_LAG)
                    elif not first:
                        pv(before, G - 1, q, TPB - PV_LAG + s)
                    if togo and not prep:
                        route(togo, s)
                    for c in range(CPB):
                        if prep and (togo, s) == AT_XT[c]:
                            if s > AT_G:
                                pe.wait_ge(s_nlo, G + 3)
                            else:
                                pe.wait_ge(s_xlo, prep * CPB + c)
                            x_transposes(prep, c)
                    if first and s == AT_WO:
                        wo_transposes()
                    if first and s == AT_M:
                        fold_m()
                    if s == AT_Y and not first:
                        if following:
                            pe.wait_ge(s_nlo, G + 2)
                        if prep and togo in (2, 3):
                            pe.wait_ge(s_xlo, prep * CPB + 8 - 2 * togo)
                        project(G - 1, head)
                    if s == AT_G and queries_:
                        if first:
                            pe.wait_ge(s_mlo, 1)
                            pe.wait_ge(s_pick, 2)
                        else:
                            pe.wait_ge(s_yadd, G)
                        queries(after2, G + 2, p, col)
                    if s == AT_MAX and following:
                        if not first and not queries_:
                            pe.wait_ge(s_yadd, G)
                        max_transposes(G + 1)

            weight_transposes()
            pe.wait_ge(s_wf, 1)
            x_transposes(0, 0)
            x_transposes(0, 1)
            pe.wait_ge(s_wlo, 1)
            fold_a(range(2))
            x_transposes(0, 2)
            x_transposes(0, 3)
            pe.wait_ge(s_xlo, 1)
            queries(0, 0, 0, 0)
            for n in range(TPB):
                if n == 4:
                    pe.wait_ge(s_nlo, 1)
                    queries(0, 1, 1, 0)
                if n == 8:
                    fold_a(range(2, HEADS))
                if n == 2:
                    pe.wait_ge(s_xlo, CPB)
                if n < CPB:
                    pe.wait_ge(s_xhi, n + 1)
                max_scores(0, 0, 0, n, first=True)
            max_transposes(0)
            for n in range(AHEAD):
                max_scores(0, 1, 1, n)
            pe.wait_ge(s_alo, 1)
            for b in range(B):
                here = (b, b, b, b)
                phase((max(b - 1, 0), b, b, b), b * GPB, 0, HEADS - 1, 0, first=b == 0)
                with pe.Fori(0, (GPB - 1 - PREP) // 2) as i:
                    phase(here, b * GPB + i * 2 + 1, 1, (i * 2) & (HEADS - 1),
                          ((i + 1) & (TPB - TPC)) * P)
                    phase(here, b * GPB + i * 2 + 2, 0, (i * 2 + 1) & (HEADS - 1),
                          ((i + 2) & (TPB - TPC)) * P)
                following = (b + 1) % B
                for togo in range(PREP, 0, -1):
                    phase((b, b, following if togo == 1 else b, following if togo <= 2 else b),
                          (b + 1) * GPB - togo, togo % 2, (-togo - 1) % HEADS,
                          0 if togo <= 2 else N - CH, following=togo > 1 or b + 1 < B,
                          queries_=togo > 2 or b + 1 < B, prep=following, togo=togo)
            steps.gate_transposes(0)
            for tile in range(TPB - PV_LAG, TPB):
                pv(B - 1, B * GPB - 1, 1, tile)
            project(B * GPB - 1, HEADS - 1)


class Store:
    pass


def routing_store(nc, ctx):
    from concourse import mybir

    f32, f32r, u32 = mybir.dt.float32, mybir.dt.float32r, mybir.dt.uint32
    rt = Store()

    def sb(name, shape, dt=f32):
        return ctx.enter_context(nc.sbuf_tensor(name, shape, dt))

    def sem(name):
        return ctx.enter_context(nc.semaphore(name))

    for_weights = (
        ("rw1_raw", [P, FF], f32), ("rw2", [P, FT, EXPERTS], f32), ("rb2", [P, EXPERTS], f32),
        ("bias_raw", [NB, P], f32))
    rt.rw1_raw, rt.rw2, rt.rb2, rt.bias_raw = (sb(*x) for x in for_weights)
    rt.rw1_hl = sb("rw1_hl", [P, 2, FF], f32r)
    rt.biasT = sb("biasT", [P, NB])
    rt.sel = sb("sel", [GR, EXPERTS, P], f32r)
    rt.iota_u = sb("iota_u", [P, TPC, EXPERTS], mybir.dt.int32)
    rt.iota = sb("iota", [P, TPC, EXPERTS])
    rt.bn = sb("bn2", [P, TPC, 6])
    rt.mv = sb("mv2", [P, TPC, 2])
    rt.rstd = sb("rstd2", [P, TPC])
    rt.xT_hl = sb("xT_hl", [P, 2, 2, CH], f32r)
    rt.rh = sb("rh", [P, FT, CH])
    rt.s8 = sb("s8", [P, TPC, EXPERTS])
    rt.top = sb("top", [P, TPC, 8])
    rt.idx = sb("idx", [P, TPC, 8], u32)
    rt.idxf = sb("idxf", [P, TPC, 8])
    rt.is0 = sb("is0", [P, TPC, EXPERTS])
    rt.is1 = sb("is1", [P, TPC, EXPERTS])
    rt.mask = sb("mask", [P, TPC, EXPERTS])
    rt.shifted = sb("shifted", [P, TPC, EXPERTS])
    rt.e8 = sb("e8", [P, TPC, EXPERTS])
    rt.em = sb("em", [P, TPC, EXPERTS])
    rt.gsum = sb("gsum", [P, TPC])
    rt.grcp = sb("grcp", [P, TPC])
    rt.gpad = sb("gpad", [P, TPC, P])
    rt.gT = sb("gT", [GR, 2, CH], f32r)

    rt.s_pad, rt.s_io, rt.s_pass = sem("gpad_cleared"), sem("iota_ready"), sem("passed2")
    rt.s_bt, rt.s_bias = sem("bias_transposed"), sem("bias_ready")
    rt.s_rwhi, rt.s_rwlo = sem("rw1_hi"), sem("rw1_lo")
    rt.s_bn, rt.s_mv, rt.s_ve = sem("bn_stats2"), sem("mean_var2"), sem("var_eps2")
    rt.s_rstd, rt.s_xn = sem("rstd_ready2"), sem("xn_ready2")
    rt.s_xt, rt.s_xhi, rt.s_xlo = sem("x_transposed"), sem("chunk_hi"), sem("chunk_lo")
    rt.s_r, rt.s_rh = sem("router_z"), sem("router_h")
    rt.s_s, rt.s_sT, rt.s_st = sem("router_scores"), sem("sT_ready"), sem("scores_transposed")
    rt.s_s8, rt.s_top = sem("scores_ready"), sem("top_ready")
    rt.s_idx, rt.s_idf = sem("idx_ready"), sem("idxf_ready")
    rt.s_eq, rt.s_mask, rt.s_sh = sem("equal_ready"), sem("mask_ready"), sem("shifted_ready")
    rt.s_e8, rt.s_em, rt.s_gs = sem("gate_exp"), sem("gate_masked"), sem("gate_sum")
    rt.s_gr, rt.s_g = sem("gate_rcp"), sem("gates_ready")
    rt.s_gt, rt.s_ghi, rt.s_glo = sem("gates_transposed"), sem("gT_hi"), sem("gT_lo")
    return rt


def routing_gpsimd(pool, rt, mhalf):
    from concourse import mybir

    def power(C):
        pool.wait_ge(rt.s_ve, C + 1)
        pool.tensor_tensor(rt.rstd[:, :], rt.mv[:, :, 1], mhalf[:, 0:TPC],
                           mybir.AluOpType.pow).then_inc(rt.s_rstd, 1)

    return power


def routing_scalar(act, rt):
    from concourse import mybir

    ACT = mybir.ActivationFunctionType
    steps = Store()

    def x_hi(C, q):
        act.wait_ge(rt.s_xt, C + 1)
        act.activation(rt.xT_hl[:, q, HI, :], rt.mb[:, 0, :], ACT.Copy).then_inc(rt.s_xhi, 1)

    def router_h(C, f):
        act.wait_ge(rt.s_r, C * FT + f + 1)
        act.activation(rt.rh[:, f, :], rt.mb[:, f % 2, :], ACT.Relu,
                       bias=rt.biasT[:, EXPERTS * FT + f:EXPERTS * FT + f + 1]).then_inc(rt.s_rh, 1)

    def score(C):
        act.wait_ge(rt.s_s, C + 1)
        act.activation(rt.sT[:, :], rt.mb[0:EXPERTS, 0, :], ACT.Copy).then_inc(rt.s_sT, 1)

    def gate_exp(C):
        act.wait_ge(rt.s_sh, C + 1)
        act.activation(rt.e8[:, :, :], rt.shifted[:, :, :], ACT.Exp).then_inc(rt.s_e8, 1)

    def gate_hi(C, q):
        act.wait_ge(rt.s_gt, C + 1)
        act.activation(rt.gT[:, q, :], rt.mb[0:GR, 1, :], ACT.Copy).then_inc(rt.s_ghi, 1)

    steps.x_hi = x_hi
    steps.router_h = router_h
    steps.score = score
    steps.gate_exp = gate_exp
    steps.gate_hi = gate_hi
    return steps


def routing_vector(dve, rt, x_sb):
    import concourse.bass as bass
    from concourse import mybir

    f32 = mybir.dt.float32
    ALU, AX = mybir.AluOpType, mybir.AxisListType
    ds = bass.ds
    steps = Store()

    def low(out, x, hi, done):
        dve.tensor_tensor(out, x, hi.bitcast(f32), ALU.subtract).then_inc(done, 1)

    def tile(C, u):
        return x_sb[:, ds(C * TPC + u, 1), :].rearrange("p a d -> p (a d)")

    def moments(C, step):
        if step == 0:
            for u in range(TPC):
                last = dve.bn_stats(rt.bn[:, u, :], tile(C, u))
            last.then_inc(rt.s_bn, 1)
        if step == 1:
            dve.wait_ge(rt.s_bn, C + 1)
            dve.sem_inc(rt.s_pass, 1)
            for u in range(TPC):
                last = dve.bn_aggr(rt.mv[:, u, :], rt.bn[:, u, :])
            last.then_inc(rt.s_mv, 1)
        if step == 2:
            dve.wait_ge(rt.s_mv, C + 1)
            dve.tensor_scalar(rt.mv[:, :, 1], rt.mv[:, :, 1], EPS, None, ALU.add).then_inc(rt.s_ve, 1)

    def normalise(C, u):
        if u == 0:
            dve.wait_ge(rt.s_rstd, C + 1)
        dve.tensor_scalar(rt.xn[:, u * D:(u + 1) * D], tile(C, u), rt.mv[:, u, 0:1],
                          rt.rstd[:, u:u + 1], ALU.subtract, ALU.mult).then_inc(rt.s_xn, 1)

    def x_lo(C, q):
        dve.wait_ge(rt.s_xhi, C + 1)
        low(rt.xT_hl[:, q, LO, :], rt.mb[:, 0, :], rt.xT_hl[:, q, HI, :], rt.s_xlo)

    def over(a):
        return a.to_broadcast([P, TPC, EXPERTS])

    def gates(C, step):
        if step == 0:
            dve.wait_ge(rt.s_st, C + 1)
            dve.tensor_tensor(rt.s8[:, :, :], rt.mb[:, 1, 0:TPC * EXPERTS]
                              .rearrange("p (u e) -> p u e", u=TPC),
                              rt.rb2[:, :].rearrange("p (a e) -> p a e", a=1)
                              .to_broadcast([P, TPC, EXPERTS]), ALU.add).then_inc(rt.s_s8, 1)
        if step == 1:
            dve.wait_ge(rt.s_s8, C + 1)
            dve.sem_inc(rt.s_pass, 1)
            for u in range(TPC):
                last = dve.max(rt.top[:, u, :], rt.s8[:, u, :])
            last.then_inc(rt.s_top, 1)
        if step == 2:
            dve.wait_ge(rt.s_top, C + 1)
            dve.tensor_tensor(rt.shifted[:, :, :], rt.s8[:, :, :], over(rt.top[:, :, 0:1]),
                              ALU.subtract).then_inc(rt.s_sh, 1)
            for u in range(TPC):
                last = dve.max_index(rt.idx[:, u, :], rt.top[:, u, :], rt.s8[:, u, :])
            last.then_inc(rt.s_idx, 1)
        if step == 3:
            dve.wait_ge(rt.s_idx, C + 1)
            dve.tensor_copy(rt.idxf[:, :, :], rt.idx[:, :, :]).then_inc(rt.s_idf, 1)
        if step == 4:
            dve.wait_ge(rt.s_idf, C + 1)
            dve.tensor_tensor(rt.is0[:, :, :], rt.iota[:, :, :], over(rt.idxf[:, :, 0:1]), ALU.is_equal)
            dve.tensor_tensor(rt.is1[:, :, :], rt.iota[:, :, :], over(rt.idxf[:, :, 1:2]),
                              ALU.is_equal).then_inc(rt.s_eq, 1)
        if step == 5:
            dve.wait_ge(rt.s_eq, C + 1)
            dve.tensor_tensor(rt.mask[:, :, :], rt.is0[:, :, :], rt.is1[:, :, :],
                              ALU.add).then_inc(rt.s_mask, 1)
        if step == 6:
            dve.wait_ge(rt.s_e8, C + 1)
            dve.wait_ge(rt.s_mask, C + 1)
            dve.tensor_tensor(rt.em[:, :, :], rt.e8[:, :, :], rt.mask[:, :, :], ALU.mult).then_inc(rt.s_em, 1)
        if step == 7:
            dve.wait_ge(rt.s_em, C + 1)
            dve.tensor_reduce(rt.gsum[:, :], rt.em[:, :, :], AX.X, ALU.add).then_inc(rt.s_gs, 1)
        if step == 8:
            dve.wait_ge(rt.s_gs, C + 1)
            dve.reciprocal(rt.grcp[:, :], rt.gsum[:, :]).then_inc(rt.s_gr, 1)
        if step == 9:
            dve.wait_ge(rt.s_gr, C + 1)
            r = rt.grcp[:, :].rearrange("p (u a) -> p u a", a=1)
            dve.tensor_tensor(rt.gpad[:, :, 0:EXPERTS], rt.em[:, :, :], over(r), ALU.mult)
            dve.tensor_tensor(rt.gpad[:, :, 32:32 + EXPERTS], rt.em[:, :, :], over(r),
                              ALU.mult).then_inc(rt.s_g, 1)

    def gate_lo(C, q):
        dve.wait_ge(rt.s_ghi, C + 1)
        rows = slice(32, 32 + EXPERTS)
        low(rt.gT[rows, q, :], rt.mb[rows, 1, :], rt.gT[rows, q, :], rt.s_glo)

    steps.moments = moments
    steps.normalise = normalise
    steps.x_lo = x_lo
    steps.gates = gates
    steps.gate_lo = gate_lo
    return steps


def routing_tensor(pe, rt, ident):
    steps = Store()

    def product(out, lhs, rhs, start, stop):
        pe.matmul(out, lhs(HI), rhs(HI), start=start, stop=False)
        pe.matmul(out, lhs(HI), rhs(LO), start=False, stop=False)
        return pe.matmul(out, lhs(LO), rhs(HI), start=False, stop=stop)

    def x_transposes(C):
        pe.wait_ge(rt.s_xn, (C + 1) * TPC)
        for u in range(TPC):
            last = pe.transpose(rt.mb[:, 0, u * P:(u + 1) * P], rt.xn[:, u * D:(u + 1) * D], ident[:, :])
        last.then_inc(rt.s_xt, 1)

    def router(C, q, f):
        if f == 0:
            pe.wait_ge(rt.s_xlo, C + 1)
        if f >= 2:
            pe.wait_ge(rt.s_rh, C * FT + f - 1)
        product(rt.mb[:, f % 2, :], lambda a: rt.rw1_hl[:, a, f * P:(f + 1) * P],
                lambda a: rt.xT_hl[:, q, a, :], True, True).then_inc(rt.s_r, 1)

    def score(C):
        pe.wait_ge(rt.s_rh, (C + 1) * FT)
        for f in range(FT):
            last = pe.matmul(rt.mb[0:EXPERTS, 0, :], rt.rw2[:, f, :], rt.rh[:, f, :],
                             start=f == 0, stop=f == FT - 1)
        last.then_inc(rt.s_s, 1)

    def score_transposes(C):
        pe.wait_ge(rt.s_sT, C + 1)
        pe.sem_inc(rt.s_pass, 1)
        for u in range(TPC):
            last = pe.transpose(rt.mb[:, 1, u * EXPERTS:(u + 1) * EXPERTS],
                                rt.sT[:, u * P:(u + 1) * P], ident[0:EXPERTS, 0:EXPERTS])
        last.then_inc(rt.s_st, 1)

    def gate_transposes(C):
        pe.wait_ge(rt.s_g, C + 1)
        for u in range(TPC):
            last = pe.transpose(rt.mb[:, 1, u * P:(u + 1) * P], rt.gpad[:, u, :], ident[:, :])
        last.then_inc(rt.s_gt, 1)

    steps.x_transposes = x_transposes
    steps.router = router
    steps.score = score
    steps.score_transposes = score_transposes
    steps.gate_transposes = gate_transposes
    return steps


def experts(nc, t, rt):
    import concourse.bass as bass
    from concourse import mybir
    from contextlib import ExitStack

    f32, f32r = mybir.dt.float32, mybir.dt.float32r
    ALU, ACT = mybir.AluOpType, mybir.ActivationFunctionType
    ds = bass.ds
    x_sb, ident = t["x_sb"], t["ident"]
    w1_raw, b2_raw = t["w1_raw"], t["b2_raw"]
    SLOTS = EXPERTS * FT
    LAG = 5
    RING = 8
    AT_XT, AT_R, AT_S, AT_ST, AT_G, AT_GT = 9, (13, 14, 15, 16), 18, 20, 21, 28

    with ExitStack() as ctx:
        def sb(name, shape, dt=f32):
            return ctx.enter_context(nc.sbuf_tensor(name, shape, dt))

        def pb(name, shape):
            return ctx.enter_context(nc.psum_tensor(name, shape, f32))

        def sem(name):
            return ctx.enter_context(nc.semaphore(name))

        w1_hl = sb("w1_hl", [P, 2, EXPERTS, FF], f32r)
        w2_hl = sb("w2_hl", [P, 2, EXPERTS, FF], f32r)
        b2_hl = sb("b2_hl", [GR, 2, D], f32r)
        w2_raw = sb("w2_raw", [P, EXPERTS, FF])
        mhalf = sb("mhalf2", [P, TPC])
        rt.xn = sb("xn2", [P, CH])
        rt.sT = sb("sT", [EXPERTS, CH])
        biasT, xT_hl, gT, sel = rt.biasT, rt.xT_hl, rt.gT, rt.sel
        gbc = sb("gbc", [P, 2, CH])
        tt = sb("tt", [P, 4, CH])
        h_hl = sb("h_hl", [P, RING, 2, CH], f32r)
        y_sb = sb("y_sb", [P, CH])

        zb = pb("zb", [P, 4, CH])
        yb = pb("yb", [P, CH])
        gb = pb("gb", [P, CH])
        rt.mb = mb = pb("mb", [P, 2, CH])

        s_mh, s_w2a, s_w2b = sem("mhalf_ready2"), sem("w2_first_loaded"), sem("w2_loaded")
        s_w1f = sem("w1_first_lo")
        s_b2hi, s_b2lo = sem("b2_hi"), sem("b2_lo")
        s_w1hi, s_w1lo, s_w2hi, s_w2lo = sem("w1_hi"), sem("w1_lo"), sem("w2_hi"), sem("w2_lo")
        s_gb, s_gbc = sem("gate_spread"), sem("gbc_ready")
        s_z, s_tt, s_hhi, s_hlo, s_w2 = (sem(n) for n in (
            "z_done", "tt_ready", "h_hi", "h_lo", "second_done"))
        s_y, s_ysb, s_yt, s_yadd = sem("y_chunk"), sem("y_in_sbuf"), sem("y_transposed"), sem("y_added2")
        s_out = sem("out_stored")

        block = ctx.enter_context(nc.Block())

        @block.sync
        def _(sp):
            w2 = w2_raw[:, :, :].rearrange("p e (f d) -> p (e f) d", f=FT)
            src = t["W2"].rearrange("e (f p) d -> p (e f) d", p=P)
            sp.dma_start(w2[:, 0:FT, :], src[:, 0:FT, :]).then_inc(s_w2a, 16)
            sp.dma_start(w2[:, FT:, :], src[:, FT:, :]).then_inc(s_w2b, 16)
            out = t["out"].rearrange("b n d -> (b n) d")
            with sp.Fori(0, CHUNKS) as c:
                sp.wait_ge(s_yadd, c + 1)
                sp.dma_start(out[ds(c * CH, CH), :].rearrange("(u p) d -> p u d", p=P),
                             x_sb[:, ds(c * TPC, TPC), :]).then_inc(s_out, 16)
            sp.wait_ge(s_out, 16 * CHUNKS)

        @block.gpsimd
        def _(pool):
            pool.memset(mhalf[:, :], -0.5).then_inc(s_mh, 1)
            pool.wait_ge(s_mh, 1)

            power = routing_gpsimd(pool, rt, mhalf)
            for e in range(1, EXPERTS + 1):
                for raw, hl, hi, lo, expert in ((w1_raw, w1_hl, s_w1hi, s_w1lo, e),
                                                (w2_raw, w2_hl, s_w2hi, s_w2lo, e - 1)):
                    if expert < EXPERTS:
                        pool.wait_ge(hi, expert + 1)
                        pool.tensor_tensor(hl[:, LO, expert, :], raw[:, expert, :],
                                           hl[:, HI, expert, :].bitcast(f32),
                                           ALU.subtract).then_inc(lo, 1)
                if e == 1:
                    power(1)
            with pool.Fori(2, CHUNKS) as c:
                power(c)

        @block.scalar
        def _(act):
            steps = routing_scalar(act, rt)

            def gate_copy(C, e):
                act.wait_ge(s_gb, C * EXPERTS + e + 1)
                act.activation(gbc[:, e % 2, :], gb[:, :], ACT.Copy).then_inc(s_gbc, 1)

            def w1_hi(e):
                act.activation(w1_hl[:, HI, e, :], w1_raw[:, e, :], ACT.Copy).then_inc(s_w1hi, 1)

            def w2_hi(e):
                act.wait_ge(s_w2a if e == 0 else s_w2b, 16)
                act.activation(w2_hl[:, HI, e, :], w2_raw[:, e, :], ACT.Copy).then_inc(s_w2hi, 1)

            w1_hi(0)
            gate_copy(0, 0)
            w1_hi(1)
            w1_hi(2)
            act.activation(b2_hl[:, HI, :], b2_raw[:, :], ACT.Copy).then_inc(s_b2hi, 1)

            def phase(C, p, prep=True, first=False):
                q = 1 - p
                for k in range(SLOTS):
                    act.wait_ge(s_tt, C * SLOTS + k + 1)
                    if not (first and k < RING):
                        act.wait_ge(s_w2, C * SLOTS + k - RING + 1)
                    act.activation(h_hl[:, k % RING, HI, :], tt[:, k % 4, :], ACT.Relu).then_inc(s_hhi, 1)
                    if first and k % FT == 0:
                        w2_hi(k // FT)
                        if k // FT + 3 < EXPERTS:
                            w1_hi(k // FT + 3)
                    if k % FT == 2 and k + FT < SLOTS:
                        gate_copy(C, k // FT + 1)
                    if k == 1 and not first:
                        act.wait_ge(s_y, C)
                        act.activation(y_sb[:, :], yb[:, :], ACT.Copy).then_inc(s_ysb, 1)
                    if prep:
                        if k == AT_XT:
                            steps.x_hi(C + 1, q)
                        for f in range(FT):
                            if k == AT_R[f]:
                                steps.router_h(C + 1, f)
                        if k == AT_S:
                            steps.score(C + 1)
                        if k == AT_G + 1:
                            steps.gate_exp(C + 1)
                        if k == AT_GT:
                            steps.gate_hi(C + 1, q)
                        if k == SLOTS - 1:
                            gate_copy(C + 1, 0)

            phase(0, 0, first=True)
            with act.Fori(0, (CHUNKS - 2) // 2) as i:
                phase(i * 2 + 1, 1)
                phase(i * 2 + 2, 0)
            phase(CHUNKS - 1, 1, prep=False)
            act.wait_ge(s_y, CHUNKS)
            act.activation(y_sb[:, :], yb[:, :], ACT.Copy).then_inc(s_ysb, 1)

        @block.vector
        def _(dve):
            def low(out, x, hi, done):
                dve.tensor_tensor(out, x, hi.bitcast(f32), ALU.subtract).then_inc(done, 1)

            steps = routing_vector(dve, rt, x_sb)
            dve.wait_ge(s_w1hi, 1)
            low(w1_hl[:, LO, 0, :], w1_raw[:, 0, :], w1_hl[:, HI, 0, :], s_w1f)
            dve.wait_ge(s_b2hi, 1)
            low(b2_hl[:, LO, :], b2_raw[:, :], b2_hl[:, HI, :], s_b2lo)

            def scale(C, k):
                if k % FT == 0:
                    dve.wait_ge(s_gbc, C * EXPERTS + k // FT + 1)
                dve.wait_ge(s_z, C * SLOTS + k + 1)
                dve.scalar_tensor_tensor(tt[:, k % 4, :], zb[:, k % 4, :], biasT[:, k:k + 1],
                                         gbc[:, k // FT % 2, :], ALU.add, ALU.mult).then_inc(s_tt, 1)

            def hidden_lo(C, k):
                dve.wait_ge(s_hhi, C * SLOTS + k + 1)
                dve.scalar_tensor_tensor(h_hl[:, k % RING, LO, :], tt[:, k % 4, :], 0.0,
                                         h_hl[:, k % RING, HI, :].bitcast(f32), ALU.max,
                                         ALU.subtract).then_inc(s_hlo, 1)

            def add_y(C):
                dve.wait_ge(s_yt, C + 1)
                tok = x_sb[:, ds(C * TPC, TPC), :].rearrange("p u d -> p (u d)")
                dve.tensor_tensor(tok, mb[:, 1, :], tok, ALU.add).then_inc(s_yadd, 1)

            def phase(C, p, prep=True, first=False):
                q = 1 - p
                for k in range(SLOTS):
                    scale(C, k)
                    step = 2 * (k - AT_G)
                    if prep and 0 <= step < 10:
                        steps.gates(C + 1, step)
                    if k > 0:
                        hidden_lo(C, k - 1)
                    elif not first:
                        hidden_lo(C - 1, SLOTS - 1)
                    if k == LAG + 1 and not first:
                        add_y(C - 1)
                    if prep:
                        if k < 3:
                            steps.moments(C + 1, k)
                        if 3 <= k < 3 + TPC:
                            steps.normalise(C + 1, k - 3)
                        if k == AT_XT:
                            steps.x_lo(C + 1, q)
                        if 0 <= step < 10:
                            steps.gates(C + 1, step + 1)
                        if k == AT_GT:
                            steps.gate_lo(C + 1, q)

            phase(0, 0, first=True)
            with dve.Fori(0, (CHUNKS - 2) // 2) as i:
                phase(i * 2 + 1, 1)
                phase(i * 2 + 2, 0)
            phase(CHUNKS - 1, 1, prep=False)
            hidden_lo(CHUNKS - 1, SLOTS - 1)
            add_y(CHUNKS - 1)

        @block.tensor
        def _(pe):
            def product(out, lhs, rhs, start, stop):
                pe.matmul(out, lhs(HI), rhs(HI), start=start, stop=False)
                pe.matmul(out, lhs(HI), rhs(LO), start=False, stop=False)
                return pe.matmul(out, lhs(LO), rhs(HI), start=False, stop=stop)

            steps = routing_tensor(pe, rt, ident)

            def spread(C, p, e):
                if e == 0:
                    pe.wait_ge(rt.s_glo, C + 1)
                else:
                    pe.wait_ge(s_gbc, C * EXPERTS + e)
                pe.matmul(gb[:, :], sel[:, e, :], gT[:, p, :], start=True, stop=True).then_inc(s_gb, 1)

            def first_product(C, p, k, first):
                if k % FT == 0 and first:
                    if k == 0:
                        pe.wait_ge(s_w1f, 1)
                    else:
                        pe.wait_ge(s_w1lo, k // FT)
                if not (first and k < 4):
                    pe.wait_ge(s_tt, C * SLOTS + k - 3)
                product(zb[:, k % 4, :], lambda a: w1_hl[:, a, k // FT, k % FT * P:(k % FT + 1) * P],
                        lambda a: xT_hl[:, p, a, :], True, True).then_inc(s_z, 1)

            def second_product(C, k, first):
                if k % FT == 0 and first:
                    pe.wait_ge(s_w2lo, k // FT + 1)
                if k == 0 and not first:
                    pe.wait_ge(s_ysb, C)
                pe.wait_ge(s_hlo, C * SLOTS + k + 1)
                product(yb[:, :], lambda a: w2_hl[:, a, k // FT, k % FT * D:(k % FT + 1) * D],
                        lambda a: h_hl[:, k % RING, a, :], k == 0, False).then_inc(s_w2, 1)

            def finish(C, p):
                pe.matmul(yb[:, :], b2_hl[:, HI, :], gT[:, p, :], start=False, stop=False)
                pe.matmul(yb[:, :], b2_hl[:, LO, :], gT[:, p, :], start=False, stop=True).then_inc(s_y, 1)

            def y_transposes(C):
                pe.wait_ge(s_ysb, C + 1)
                for u in range(TPC):
                    last = pe.transpose(mb[:, 1, u * P:(u + 1) * P], y_sb[:, u * P:(u + 1) * P], ident[:, :])
                last.then_inc(s_yt, 1)

            def phase(C, p, prep=True, first=False):
                q = 1 - p
                for k in range(SLOTS):
                    first_product(C, p, k, first)
                    if k % FT == 2 and k + FT < SLOTS:
                        spread(C, p, k // FT + 1)
                    if k >= LAG:
                        second_product(C, k - LAG, first)
                    elif not first:
                        second_product(C - 1, SLOTS - LAG + k, False)
                        if k == LAG - 1:
                            finish(C - 1, q)
                    if k == LAG + 1 and not first:
                        y_transposes(C - 1)
                    if prep:
                        if k == AT_XT:
                            steps.x_transposes(C + 1)
                        for f in range(FT):
                            if k == AT_R[f]:
                                if f == 1 and not first:
                                    pe.wait_ge(s_yadd, C)
                                steps.router(C + 1, q, f)
                        if k == AT_S:
                            steps.score(C + 1)
                        if k == AT_ST:
                            steps.score_transposes(C + 1)
                        if k == AT_GT:
                            steps.gate_transposes(C + 1)
                        if k == SLOTS - 1:
                            spread(C + 1, q, 0)

            spread(0, 0, 0)
            phase(0, 0, first=True)
            pe.wait_ge(s_w2lo, EXPERTS)
            pe.wait_ge(s_b2lo, 1)
            with pe.Fori(0, (CHUNKS - 2) // 2) as i:
                phase(i * 2 + 1, 1)
                phase(i * 2 + 2, 0)
            phase(CHUNKS - 1, 1, prep=False)
            for k in range(SLOTS - LAG, SLOTS):
                second_product(CHUNKS - 1, k, False)
            finish(CHUNKS - 1, 1)
            y_transposes(CHUNKS - 1)


def build(nc, t):
    from concourse import mybir
    from contextlib import ExitStack

    f32 = mybir.dt.float32
    with ExitStack() as ctx:
        t["x_sb"] = ctx.enter_context(nc.sbuf_tensor("x_sb", [P, TILES, D], f32))
        t["ident"] = ctx.enter_context(nc.sbuf_tensor("ident", [P, P], f32))
        t["w1_raw"] = ctx.enter_context(nc.sbuf_tensor("w1_raw", [P, EXPERTS, FF], f32))
        t["b2_raw"] = ctx.enter_context(nc.sbuf_tensor("b2_raw", [GR, D], f32))
        rt = routing_store(nc, ctx)
        attention(nc, t, rt)
        experts(nc, t, rt)


_INS = {"L0_attn_x": "x", "L0_attn_proj_q": "wq", "L0_attn_proj_k": "wk", "L0_attn_proj_v": "wv",
        "L0_attn_proj_o": "wo", "L0_ffn_rw1": "rw1", "L0_ffn_rb1": "rb1", "L0_ffn_rw2": "rw2",
        "L0_ffn_rb2": "rb2", "L0_ffn_W1": "W1", "L0_ffn_b1": "b1", "L0_ffn_W2": "W2", "L0_ffn_b2": "b2"}


def kernel(**inputs):
    import concourse.bacc as bacc
    from concourse import mybir
    from concourse.bass_utils import run_bass_kernel_spmd as run

    nc = bacc.Bacc("TRN2", target_bir_lowering=False, num_devices=1)
    arrays, t = {}, {}
    for name, short in _INS.items():
        a = np.ascontiguousarray(inputs[name])
        arrays[name] = a
        t[short] = nc.dram_tensor(name, a.shape, mybir.dt.from_np(a.dtype), kind="ExternalInput").ap()
    t["out"] = nc.dram_tensor("out", (B, N, D), mybir.dt.float32, kind="ExternalOutput").ap()
    build(nc, t)
    return run(nc, [arrays], core_ids=[0]).results[0]["out"]
```
